# Optimizing a Trainium2 kernel written in Bass

```python
import numpy as np
import jax
import jax.numpy as jnp

def _softmax(x, axis=-1):
    return jax.nn.softmax(x, axis=axis)

def _gelu(x):
    return jax.nn.gelu(x, approximate=True)

def _silu(x):
    return jax.nn.silu(x)

def _sigmoid(x):
    return jax.nn.sigmoid(x)

def _layernorm(x, axis=-1, eps=1e-05):
    m = jnp.mean(x, axis=axis, keepdims=True)
    v = jnp.var(x, axis=axis, keepdims=True)
    return (x - m) / jnp.sqrt(v + eps)

def _scatter_add(tgt, idx, src, axis=0):
    return tgt.at[idx].add(src)

def _segment_sum(src, seg, n):
    return jax.ops.segment_sum(src, seg, n)
kernel_name = 'mk_adj_preln_d2_adj_r2_2b9f6e'

def setup_inputs(seed: int=0):
    np.random.seed(seed)
    _w = jnp.asarray

    def _rec_inputs():
        import jax
        import jax.numpy as jnp
        _gk = jax.random.key(seed)
        x = -0.0005963 + 1.001 * jax.random.normal(jax.random.fold_in(_gk, 1), (3327, 256), jnp.float32)
        _a = jax.random.bernoulli(jax.random.fold_in(_gk, 2), 0.00480914, (3327, 3327))
        _a = jnp.logical_or(_a, jnp.swapaxes(_a, -1, -2))
        _a = jnp.logical_or(_a, jnp.eye(3327, dtype=bool))
        _af = _a.astype(jnp.float32)
        adj = _af
        return (x, adj)
    x, adj = _rec_inputs()

    def _L0_gnn_setup():
        import jax, jax.numpy as jnp
        import numpy as np
        N = 3072
        D_IN = 256
        D_OUT = 256
        DENSITY = 0.005
        key = jax.random.key(seed)
        ks = jax.random.split(key, 12)
        x = jax.random.normal(ks[0], (N, D_IN), dtype=jnp.float32)
        adj_a = (jax.random.uniform(ks[1], (N, N)) < DENSITY).astype(jnp.float32)
        adj_b = (jax.random.uniform(ks[2], (N, N)) < DENSITY).astype(jnp.float32)
        W_sa = jax.random.normal(ks[3], (D_IN, D_OUT), dtype=jnp.float32) * (1.414 / np.sqrt(D_IN + D_OUT))
        a_sa = jax.random.normal(ks[4], (1, 2 * D_OUT), dtype=jnp.float32) * (1.414 / np.sqrt(1 + 2 * D_OUT))
        stdv = 1.0 / np.sqrt(D_OUT)
        W_gcnb = jax.random.uniform(ks[5], (D_IN, D_OUT), minval=-stdv, maxval=stdv, dtype=jnp.float32)
        b_gcnb = jax.random.uniform(ks[6], (D_OUT,), minval=-stdv, maxval=stdv, dtype=jnp.float32)
        s = 1.0 / np.sqrt(2 * D_IN)
        Wa = jax.random.uniform(ks[7], (1, 2 * D_IN), minval=-s, maxval=s, dtype=jnp.float32)
        ba = jax.random.uniform(ks[8], (1,), minval=-s, maxval=s, dtype=jnp.float32)
        Wb = jax.random.uniform(ks[9], (1, 2 * D_IN), minval=-s, maxval=s, dtype=jnp.float32)
        bb = jax.random.uniform(ks[10], (1,), minval=-s, maxval=s, dtype=jnp.float32)
        return {'x': x, 'adj_a': adj_a, 'adj_b': adj_b, 'W_sa': W_sa, 'a_sa': a_sa, 'W_gcnb': W_gcnb, 'b_gcnb': b_gcnb, 'Wa': Wa, 'ba': ba, 'Wb': Wb, 'bb': bb}
    _L0_gnn_all = _L0_gnn_setup()
    _L0_gnn_in = {k: v for k, v in _L0_gnn_all.items() if k in ('W_sa', 'a_sa', 'W_gcnb', 'b_gcnb', 'Wa', 'ba', 'Wb', 'bb')}
    del _L0_gnn_all

    def _L1_gnn_setup():
        import jax, jax.numpy as jnp
        import numpy as np
        N = 8192
        D_IN = 256
        D_OUT = 256
        AVG_DEG = 32.0
        key = jax.random.key(seed)
        k1, k2, k3, k4 = jax.random.split(key, 4)
        p = AVG_DEG / N
        adjacency = (jax.random.uniform(k1, (N, N)) < p).astype(jnp.float32)
        adjacency = jnp.maximum(adjacency, adjacency.T)
        node_degree = jnp.sum(adjacency, axis=1, keepdims=True) + 1.0
        x = jax.random.normal(k2, (N, D_IN), dtype=jnp.float32)
        W = jax.random.normal(k3, (D_IN, D_OUT), dtype=jnp.float32) * (1.0 / np.sqrt(D_IN))
        b = jax.random.normal(k4, (D_OUT,), dtype=jnp.float32) * 0.01
        return {'x': x, 'adjacency': adjacency, 'node_degree': node_degree, 'W': W, 'b': b}
    _L1_gnn_all = _L1_gnn_setup()
    _L1_gnn_in = {k: v for k, v in _L1_gnn_all.items() if k in ('W', 'b')}
    del _L1_gnn_all
    return {'x': x, 'adj': adj, 'L0_gnn_W_sa': _L0_gnn_in['W_sa'], 'L0_gnn_a_sa': _L0_gnn_in['a_sa'], 'L0_gnn_W_gcnb': _L0_gnn_in['W_gcnb'], 'L0_gnn_b_gcnb': _L0_gnn_in['b_gcnb'], 'L0_gnn_Wa': _L0_gnn_in['Wa'], 'L0_gnn_ba': _L0_gnn_in['ba'], 'L0_gnn_Wb': _L0_gnn_in['Wb'], 'L0_gnn_bb': _L0_gnn_in['bb'], 'L1_gnn_W': _L1_gnn_in['W'], 'L1_gnn_b': _L1_gnn_in['b']}

def reference(x, adj, L0_gnn_W_sa, L0_gnn_a_sa, L0_gnn_W_gcnb, L0_gnn_b_gcnb, L0_gnn_Wa, L0_gnn_ba, L0_gnn_Wb, L0_gnn_bb, L1_gnn_W, L1_gnn_b):
    import jax
    import jax.numpy as jnp

    def _L0_gnn_ref(x, adj_a, adj_b, W_sa, a_sa, W_gcnb, b_gcnb, Wa, ba, Wb, bb):
        import jax, jax.numpy as jnp
        import numpy as np
        N = 3072
        D_IN = 256
        D_OUT = 256
        DENSITY = 0.005
        type_sum_a = adj_a @ x
        type_sum_b = adj_b @ x
        attn_a = jax.nn.sigmoid(jnp.concatenate([type_sum_a, x], axis=1) @ Wa.T + ba)
        attn_b = jax.nn.sigmoid(jnp.concatenate([type_sum_b, x], axis=1) @ Wb.T + bb)
        h = x @ W_sa
        Hd = h.shape[1]
        s_left = h @ a_sa[0, :Hd]
        s_right = h @ a_sa[0, Hd:]
        scores = s_left[:, None] + s_right[None, :]
        e = jnp.where(adj_a != 0, jnp.exp(-jax.nn.leaky_relu(scores, 0.01)), 0.0)
        attn = e / (jnp.sum(e, axis=1, keepdims=True) + 1e-05)
        x_a = attn @ h
        x_b = adj_b @ (x @ W_gcnb) + b_gcnb
        return jax.nn.sigmoid(attn_a * x_a + attn_b * x_b)

    def _L1_gnn_ref(x, adjacency, node_degree, W, b):
        import jax, jax.numpy as jnp
        import numpy as np
        N = 8192
        D_IN = 256
        D_OUT = 256
        AVG_DEG = 32.0
        n = adjacency.shape[0]
        a_hat = adjacency + jnp.eye(n, dtype=adjacency.dtype)
        dinv = jax.lax.rsqrt(node_degree)
        a_norm = dinv * a_hat * dinv
        pooled = a_norm @ x + x
        return jax.nn.relu(pooled @ W + b)
    deg = jnp.maximum((adj != 0).astype(jnp.float32).sum(-1), 1.0)
    h = jnp.maximum(_layernorm(x, axis=-1), 0.0)
    x = x + _L0_gnn_ref(h, adj, adj, L0_gnn_W_sa, L0_gnn_a_sa, L0_gnn_W_gcnb, L0_gnn_b_gcnb, L0_gnn_Wa, L0_gnn_ba, L0_gnn_Wb, L0_gnn_bb)
    h = jnp.maximum(_layernorm(x, axis=-1), 0.0)
    x = x + _L1_gnn_ref(h, adj, deg[..., None], L1_gnn_W, L1_gnn_b)
    return x

_drawn_inputs = setup_inputs


def setup_inputs(seed=0):
    import zlib

    import numpy as np

    out = dict(_drawn_inputs(seed))
    spreads = {}
    factors = {'L0_gnn_W_sa': 29.143,
     'L0_gnn_a_sa': 60.307,
     'L0_gnn_b_gcnb': 52.572,
     'L0_gnn_Wa': 4.933,
     'L1_gnn_b': 8.0}
    for name, (base, spread) in spreads.items():
        noise = np.random.default_rng([zlib.crc32(name.encode()), seed]).standard_normal(out[name].shape)
        drawn = base * np.exp(spread * noise) if base else spread * noise
        out[name] = jnp.asarray(drawn.astype(out[name].dtype))
    for name, factor in factors.items():
        out[name] = (out[name] * factor).astype(out[name].dtype)
    return out
```

```python
from contextlib import ExitStack

import concourse.bass as bass
from concourse import mybir

F32 = mybir.dt.float32
F16 = mybir.dt.float16
BF16 = mybir.dt.bfloat16
U32 = mybir.dt.uint32
ALU = mybir.AluOpType
ACT = mybir.ActivationFunctionType

P = 128
QUAD = 32
LN_EPS = 1e-5
SUM_EPS = 1e-5
SLOPE = 0.01


def gnn_kernel(nc, x, adj, W_sa, a_sa, W_g, b_g, Wa, ba, Wb, bb, W1, b1, out):
    N, D = x.shape
    PAIRS = -(-N // (2 * P))
    TILES = 2 * PAIRS
    QN = TILES * QUAD
    HALVES = D // P
    HW = D + 2
    ones_col = D
    GROUPS = [(0, 2), (2, 7), (7, PAIRS)]
    AGROUPS = [(0, 4), (4, 8), (8, PAIRS)]

    with ExitStack() as ctx:
        def sb(name, shape, dt=F32):
            return ctx.enter_context(nc.sbuf_tensor(name, shape, dt))

        def ps(name):
            return ctx.enter_context(nc.psum_tensor(name, [P, 512], F32))

        def sem(name):
            return ctx.enter_context(nc.semaphore(name))

        adjT_store = nc.dram_tensor("adjT_store", [PAIRS, P, PAIRS * 256], U32, kind="Internal").ap()

        xs = sb("xs", [P, TILES, D])
        h1 = [sb(f"h1_{l}", [P, TILES, HW], F16) for l in range(2)]
        h2 = [sb(f"h2_{l}", [P, TILES, D], F16) for l in range(2)]
        stage = sb("stage", [P, 2, 4, QN], BF16)
        adjT = sb("adjT", [P, PAIRS, 2, P, 2], BF16)
        Z = sb("Z", [P, PAIRS, 2, 2 * P])
        E2 = sb("E2", [P, PAIRS, 2, 2 * P], BF16)
        sl = sb("sl", [P, TILES * P])
        slp = sb("slp", [P, 2 * P])
        srw = sb("srw", [P, TILES, 4])
        sr99 = sb("sr99", [P, TILES])
        vr = sb("vr", [P, TILES])
        el = sb("el", [P, TILES])
        bst = sb("bst", [P, 2, 2, 6])
        mv = sb("mv", [P, PAIRS, 2, 2])
        ve = sb("ve", [P, PAIRS, 2])
        rstd = sb("rstd", [P, PAIRS, 2])
        nmr = sb("nmr", [P, PAIRS, 2])
        mhalf = sb("mhalf", [P, 2])
        lneps = sb("lneps", [P, 2])
        hf = sb("hf", [P, 2, 2, D])
        hT = sb("hT", [P, 2, HALVES, 2 * P])
        ident = sb("ident", [P, P])
        wsa = sb("wsa", [P, HALVES, D])
        wg = sb("wg", [P, HALVES, HW])
        w1 = sb("w1", [P, HALVES, D])
        w4 = sb("w4", [P, HALVES, 4])
        diag = sb("diag", [P, 2, P])
        ones = sb("ones", [P, P])
        arep = sb("arep", [P, 2 * D])
        prod = sb("prod", [P, 2 * HALVES, D])
        bias4 = sb("bias4", [P, 2, 4])
        bgrep = sb("bgrep", [P, D])
        b1rep = sb("b1rep", [P, D])
        Th = sb("Th", [P, 2, HW])
        AE = sb("AE", [P, 2, D])
        TTa = sb("TTa", [P, 2, HALVES, P])
        TTe = sb("TTe", [P, 2, HALVES, P])
        degm = sb("degm", [P, 2])
        dr = sb("dr", [P, TILES])
        drp = sb("drp", [P, 2])
        ssum = sb("ssum", [P, 2])
        rs = sb("rs", [P, 2])
        zg = sb("zg", [P, 2, 2])
        eg = sb("eg", [P, 2, 2])
        eg1 = sb("eg1", [P, 2, 2])
        gate = sb("gate", [P, 2, 2])
        ub = sb("ub", [P, 2, D])
        wm = sb("wm", [P, 2, D])
        wx = sb("wx", [P, 2, D])
        hp = sb("hp", [P, 2, D])
        osb = sb("osb", [P, 2, D])

        accE = [ps("accE0"), ps("accE1")]
        accA = [ps("accA0"), ps("accA1")]
        tp = ps("tp")
        dB = [ps("dB0"), ps("dB1")]
        dA = ps("dA")

        x_in = [sem(f"x_in{g}") for g in range(len(GROUPS))]
        w_in = sem("w_in")
        w2_in = sem("w2_in")
        pads = sem("pads")
        consts = sem("consts")
        id0 = sem("id0")
        wprep = sem("wprep")
        wchain = sem("wchain")
        stats = [sem(f"stats_{l}") for l in range(2)]
        bnr = [sem(f"bnr_{l}") for l in range(2)]
        vplus = [sem(f"vplus_{l}") for l in range(2)]
        rstd_ok = [sem(f"rstd_ok_{l}") for l in range(2)]
        nmr_ok = [sem(f"nmr_ok_{l}") for l in range(2)]
        hf_ok = [sem(f"hf_ok_{l}") for l in range(2)]
        h1_ok = [sem(f"h1_ok_{l}") for l in range(2)]
        h2_ok = sem("h2_ok")
        hT_ps = sem("hT_ps")
        hT_ok = sem("hT_ok")
        proj = sem("proj")
        diag_ok = sem("diag_ok")
        wide = sem("wide")
        srw_ok = sem("srw_ok")
        sl_ok = sem("sl_ok")
        adj_in = sem("adj_in")
        tr_done = sem("tr_done")
        stored = sem("stored")
        a_done = sem("a_done")
        slp_ok = sem("slp_ok")
        vr_ok = sem("vr_ok")
        sr99_ok = sem("sr99_ok")
        pl_ok = sem("pl_ok")
        exp_ok = sem("exp_ok")
        mask_ok = sem("mask_ok")
        e2_ok = sem("e2_ok")
        unit_done = sem("unit_done")
        th_ok = sem("th_ok")
        deg_c = sem("deg_c")
        deg_ok = sem("deg_ok")
        tp_w = sem("tp_w")
        tp_ev = sem("tp_ev")
        db_ok = sem("db_ok")
        da_ok = sem("da_ok")
        rs_c = sem("rs_c")
        rs_ok = sem("rs_ok")
        ae_ok = sem("ae_ok")
        zg_ok = sem("zg_ok")
        eg_ok = sem("eg_ok")
        gate_c = sem("gate_c")
        gate_ok = sem("gate_ok")
        ub_ok = sem("ub_ok")
        wm_c = sem("wm_c")
        wm_ok = sem("wm_ok")
        wx_ok = sem("wx_ok")
        x1_c = sem("x1_c")
        x1_ok = sem("x1_ok")
        adj_ld = [sem(f"adj_ld{g}") for g in range(len(AGROUPS))]
        grp_done = [sem(f"grp_done{g}") for g in range(len(AGROUPS))]
        hp_ok = sem("hp_ok")
        pt_c = sem("pt_c")
        pool_ok = sem("pool_ok")
        drp_ok = sem("drp_ok")
        l1t_w = sem("l1t_w")
        l1t_ev = sem("l1t_ev")
        l1d_ok = sem("l1d_ok")
        ob_c = sem("ob_c")
        o_ok = sem("o_ok")
        o_out = sem("o_out")

        N_WDMA = 8
        N_W2DMA = 6

        block = ctx.enter_context(nc.Block())

        @block.sync
        def _(sp):
            sp.wait_ge(pads, 2)
            for g, (u0, u1) in enumerate(GROUPS):
                for b in range(4):
                    full = u1 if (b < 3 or u1 < PAIRS) else PAIRS - 1
                    src = bass.AP(x.tensor, (QN * b + 64 * u0) * D,
                                  [[2 * D, QUAD], [64 * D, full - u0], [1, 2 * D]])
                    dst = xs[32 * b:32 * b + 32, 2 * u0:2 * full, :].rearrange("p (u v) d -> p u (v d)", v=2)
                    sp.dma_start(dst, src).then_inc(x_in[g], 16)
                    if full < u1:
                        r0 = QN * b + 64 * full
                        src = bass.AP(x.tensor, r0 * D, [[2 * D, QUAD - 1], [1, 2 * D]])
                        dst = xs[96:96 + QUAD - 1, 2 * full:2 * u1, :].rearrange("p v d -> p (v d)")
                        sp.dma_start(dst, src).then_inc(x_in[g], 16)
                        src = bass.AP(x.tensor, (N - 1) * D, [[D, 1], [1, D]])
                        sp.dma_start(xs[P - 1:P, 2 * full, :], src).then_inc(x_in[g], 16)
            sp.dma_start(wg[:, :, 0:D], W_g.rearrange("(h p) o -> p h o", p=P)).then_inc(w2_in, 16)
            sp.dma_start(bgrep[:], bass.AP(b_g.tensor, 0, [[0, P], [1, D]])).then_inc(w2_in, 16)
            sp.dma_start(w1[:], W1.rearrange("(h p) o -> p h o", p=P)).then_inc(w2_in, 16)
            sp.dma_start(b1rep[:], bass.AP(b1.tensor, 0, [[0, P], [1, D]])).then_inc(w2_in, 16)
            with sp.Fori(0, PAIRS) as q:
                sp.wait_ge(tr_done, q + 1)
                sp.dma_start(adjT_store[bass.ds(q, 1)].rearrange("a p n -> p (a n)"),
                             adjT[:].rearrange("p u e i v -> p (u e i v)").bitcast(U32)).then_inc(stored, 16)
            sp.wait_ge(stored, 16 * PAIRS)

            def load_pair(q):
                for g, (u0, u1) in enumerate(AGROUPS):
                    yield g, (adjT[:, u0:u1].rearrange("p u e i v -> p (u e i v)").bitcast(U32),
                              adjT_store[bass.ds(q, 1), :, 256 * u0:256 * u1].rearrange("a p n -> p (a n)"))

            sp.wait_ge(mask_ok, PAIRS * PAIRS)
            sp.wait_ge(a_done, TILES)
            for g, (dst, src) in load_pair(0):
                sp.dma_start(dst, src).then_inc(adj_ld[g], 16)

            with sp.Fori(0, PAIRS - 1) as q:
                for g, (dst, src) in load_pair(q + 1):
                    sp.wait_ge(grp_done[g], q + 1)
                    sp.dma_start(dst, src).then_inc(adj_ld[g], 16)

        @block.gpsimd
        def _(pool):
            pool.memset(ident[:], 0.0).then_inc(id0, 1)
            pool.memset(ones[:], 1.0).then_inc(consts, 1)
            pool.memset(mhalf[:], -0.5).then_inc(consts, 1)
            pool.memset(lneps[:], LN_EPS).then_inc(consts, 1)
            for l in range(2):
                pool.memset(h1[l][:, :, ones_col:HW], 1.0).then_inc(consts, 1)
            pool.wait_ge(id0, 1)
            pool.affine_select(out=ident[:], in_=ident[:], compare_op=ALU.not_equal, fill=1.0, base=0,
                               pattern=[[-1, P]], channel_multiplier=1).then_inc(consts, 1)

            def load_adj(q, last=False, quadrants=range(4)):
                for b in quadrants:
                    w = QN if b < 3 else QN - 1
                    for e in range(2):
                        short = last and e == 1
                        base = q * (64 * N) + (e * N + QN * b)
                        dst = stage[32 * b:32 * b + 32, e]
                        src = bass.AP(adj.tensor, base, [[2 * N, QUAD], [QN * N, 3 if short else 4], [1, w]])
                        pool.dma_start(dst[:, 0:3 if short else 4, 0:w], src).then_inc(adj_in, 16)
                        if short:
                            src = bass.AP(adj.tensor, base + 3 * QN * N, [[2 * N, QUAD - 1], [1, w]])
                            pool.dma_start(dst[0:QUAD - 1, 3, 0:w], src).then_inc(adj_in, 16)

            def inv_std(i, par, l):
                pool.wait_ge(stats[l], i + 1)
                pool.tensor_tensor(ve[:, par], mv[:, par, :, 1], lneps[:], ALU.add).then_inc(vplus[l], 1)
                pool.wait_ge(vplus[l], i + 1)
                if l:
                    pool.wait_ge(h2_ok, PAIRS + i)
                pool.tensor_tensor(rstd[:, par], ve[:, par], mhalf[:], ALU.pow).then_inc(rstd_ok[l], 1)

            def first_part(i, par, l, dst):
                pool.wait_ge(hf_ok[l], 2 * i + 2)
                pool.tensor_copy(dst, hf[:, par]).then_inc(h1_ok[l], 1)

            def later_first(q):
                first_part(q, 0, 1, h1[1][:, bass.ds(2 * q, 2), 0:D])

            pool.wait_ge(pads, 1)
            load_adj(0, quadrants=(0, 1))
            pool.wait_ge(consts, 6)
            inv_std(0, 0, 0)
            load_adj(0, quadrants=(2, 3))
            inv_std(1, 1, 0)
            for i in range(PAIRS):
                if i + 2 < PAIRS:
                    inv_std(i + 2, i + 2, 0)
                first_part(i, i % 2, 0, h1[0][:, 2 * i:2 * i + 2, 0:D])

            pool.wait_ge(tr_done, 1)
            load_adj(1)
            pool.wait_ge(tr_done, 2)
            load_adj(2)
            with pool.Fori(0, PAIRS - 4) as q:
                inv_std(q, 0, 1)
                pool.wait_ge(tr_done, q + 3)
                load_adj(q + 3)
                later_first(q)
            inv_std(PAIRS - 4, 0, 1)
            pool.wait_ge(tr_done, PAIRS - 1)
            pool.memset(stage[:, 1, 3, :], 0.0).then_inc(pads, 1)
            pool.wait_ge(pads, 3)
            load_adj(PAIRS - 1, last=True)
            later_first(PAIRS - 4)
            for q in range(PAIRS - 3, PAIRS):
                inv_std(q, 0, 1)
                later_first(q)

            def self_h(q):
                pool.tensor_tensor(hp[:], h1[1][:, bass.ds(2 * q, 2), 0:D], h2[1][:, bass.ds(2 * q, 2), :],
                                   ALU.add).then_inc(hp_ok, 1)
            pool.wait_ge(h2_ok, 2 * PAIRS)
            self_h(0)
            with pool.Fori(0, PAIRS - 1) as q:
                pool.wait_ge(pool_ok, 2 * q + 2)
                self_h(q + 1)

        @block.scalar
        def _(act):
            def wdma(dst, src, scattered=False):
                act.dma_start(dst, src, allow_slow_non_contiguous=scattered).then_inc(w_in, 16)

            rep = lambda t, off, n: bass.AP(t.tensor, off, [[0, P], [1, n]])
            wdma(wsa[:], W_sa.rearrange("(h p) o -> p h o", p=P))
            wdma(arep[:], rep(a_sa, 0, 2 * D))
            for k, w in enumerate((Wa, Wb)):
                wdma(w4[:, :, 1 + k], w[0, D:2 * D].rearrange("(h p) -> p h", p=P), True)
            for e in range(2):
                wdma(bias4[:, e, 1:2], rep(ba, 0, 1))
                wdma(bias4[:, e, 2:3], rep(bb, 0, 1))
            for k, w in enumerate((Wa, Wb)):
                act.dma_start(wg[:, :, D + k], w[0, 0:D].rearrange("(h p) -> p h", p=P),
                              allow_slow_non_contiguous=True).then_inc(w2_in, 16)

            def norm(i, slot, par, l, src):
                if l:
                    act.wait_ge(hT_ps, PAIRS)
                act.wait_ge(nmr_ok[l], i + 1)
                for e in range(2):
                    act.activation(hf[:, par, e], src[:, e], ACT.Relu, bias=nmr[:, slot, e:e + 1],
                                   scale=rstd[:, slot, e:e + 1]).then_inc(hf_ok[l], 1)

            def leaky(m, u, fresh):
                if not fresh:
                    act.wait_ge(unit_done, (m - 1) * PAIRS + (u + 1))
                for v in range(2):
                    t = 2 * u + v
                    ins = act.activation(Z[:, u, v], slp[:], ACT.Relu, bias=sr99[:, t:t + 1], scale=1.0 - SLOPE)
                ins.then_inc(pl_ok, 1)

            def expo(m, u):
                act.wait_ge(pl_ok, m * PAIRS + (u + 1))
                act.activation(Z[:, u], Z[:, u], ACT.Exp, scale=-1.0).then_inc(exp_ok, 1)

            for i in range(PAIRS + 4):
                if i < PAIRS:
                    act.wait_ge(x_in[[g for g, (a, b) in enumerate(GROUPS) if a <= i < b][0]],
                                16 * (4 if i < GROUPS[-1][0] else 6))
                    if i >= 2:
                        act.wait_ge(h2_ok, i - 1)
                        act.wait_ge(hT_ps, i - 1)
                    norm(i, i, i % 2, 0, xs[:, 2 * i:2 * i + 2])
                j = i - 1
                if 0 <= j < PAIRS:
                    act.wait_ge(hT_ps, j + 1)
                    if j >= 2:
                        act.wait_ge(proj, j - 1)
                    act.activation(hT[:, j % 2], [tp, dA][j % 2][:].rearrange("p (h n) -> p h n", h=HALVES),
                                   ACT.Copy).then_inc(hT_ok, 1)
                j = i - 3
                if 0 <= j < PAIRS:
                    act.wait_ge(srw_ok, j + 1)
                    act.activation(vr[:, 2 * j:2 * j + 2], srw[:, 2 * j:2 * j + 2, 0], ACT.Exp,
                                   scale=-SLOPE).then_inc(vr_ok, 1)
                    act.wait_ge(wide, j + 1)
                    act.activation(sl[:, 2 * P * j:2 * P * (j + 1)], dB[1][:, 0:2 * P],
                                   ACT.Copy).then_inc(sl_ok, 1)
                    if j == 0:
                        act.wait_ge(sl_ok, 1)
                        act.activation(slp[:], sl[:, 0:2 * P], ACT.Copy).then_inc(slp_ok, 1)
                        act.wait_ge(slp_ok, 1)
                    act.wait_ge(sr99_ok, j + 1)
                    leaky(0, j, True)
                j = i - 4
                if 0 <= j < PAIRS:
                    expo(0, j)
            act.activation(el[:], srw[:, :, 3], ACT.Exp, scale=SLOPE).then_inc(vr_ok, 1)
            act.wait_ge(sl_ok, PAIRS)


            def sums_out(m, e):
                act.wait_ge(a_done, 2 * m + (e + 1))
                if e == 0:
                    act.wait_ge(deg_ok, m)
                    act.wait_ge(tp_w, 2 * m)
                act.activation(Th[:, e, 0:D + 1], accA[e][:, 0:D + 1], ACT.Copy).then_inc(th_ok, 1)

            def turned_a(m):
                act.wait_ge(tp_w, 2 * m + 1)
                act.wait_ge(db_ok, m)
                act.activation(TTa[:].rearrange("p e h i -> p (e h i)"), tp[:], ACT.Copy).then_inc(tp_ev, 1)

            def attn_out(q):
                act.wait_ge(rs_ok, q + 1)
                for e in range(2):
                    act.activation(AE[:, e], accE[e][:, 0:D], ACT.Copy, scale=rs[:, e:e + 1]).then_inc(ae_ok, 1)

            def turned_e(q):
                act.wait_ge(tp_w, 2 * q + 2)
                act.activation(TTe[:].rearrange("p e h i -> p (e h i)"), tp[:], ACT.Copy).then_inc(tp_ev, 1)

            def gate_exp(q):
                act.wait_ge(zg_ok, q + 1)
                act.activation(eg[:], zg[:], ACT.Exp, scale=-1.0).then_inc(eg_ok, 1)

            def gated_b(q):
                act.wait_ge(gate_ok, q + 1)
                act.wait_ge(db_ok, q + 1)
                for e in range(2):
                    act.activation(ub[:, e], dB[e][:, 0:D], ACT.Copy, scale=gate[:, e, 1:2]).then_inc(ub_ok, 1)

            def half_tanh(q):
                act.wait_ge(wm_ok, 2 * q + 2)
                act.activation(wx[:], wm[:], ACT.Tanh, scale=0.5).then_inc(wx_ok, 1)

            def norm_later(q):
                act.wait_ge(x1_ok, q + 1)
                act.wait_ge(h2_ok, PAIRS + q)
                norm(q, 0, 0, 1, xs[:, bass.ds(2 * q, 2)])

            def layer0(m, q, p):
                act.activation(slp[:], sl[:, bass.ds(m * (2 * P), 2 * P)], ACT.Copy).then_inc(slp_ok, 1)
                act.wait_ge(slp_ok, m + 1)
                for u in range(PAIRS + 1):
                    if u < PAIRS:
                        leaky(m, u, False)
                    if u >= 1:
                        expo(m, u - 1)
                    if p is not None and u == 3:
                        norm_later(p)
                    if u == 11:
                        attn_out(q)
                        gate_exp(q)
                gated_b(q)
                sums_out(m, 0)
                turned_e(q)
                sums_out(m, 1)
                half_tanh(q)
                turned_a(m)

            sums_out(0, 0)
            sums_out(0, 1)
            turned_a(0)
            layer0(1, 0, None)
            with act.Fori(0, PAIRS - 2) as q:
                layer0(q + 2, q + 1, q)
            last = PAIRS - 1
            norm_later(last - 1)
            attn_out(last)
            gate_exp(last)
            gated_b(last)
            turned_e(last)
            half_tanh(last)
            norm_later(last)

            def turned_p(q):
                act.wait_ge(l1t_w, q + 1)
                act.activation(TTa[:].rearrange("p e h i -> p (e h i)"), tp[:], ACT.Copy).then_inc(l1t_ev, 1)
            def store_out(q, rows=QUAD):
                for b in range(4):
                    k = rows if b == 3 else QUAD
                    dst = bass.AP(out.tensor, (QN * b) * D + q * (64 * D), [[2 * D, k], [1, 2 * D]])
                    act.dma_start(dst, osb[32 * b:32 * b + k].rearrange("p e d -> p (e d)")).then_inc(o_out, 16)

            turned_p(0)
            with act.Fori(0, PAIRS - 1) as q:
                act.wait_ge(o_ok, q + 1)
                store_out(q)
                turned_p(q + 1)
            act.wait_ge(o_ok, PAIRS)
            store_out(PAIRS - 1, QUAD - 1)
            dst = bass.AP(out.tensor, (N - 1) * D, [[D, 1], [1, D]])
            act.dma_start(dst, osb[P - 1:P, 0, :]).then_inc(o_out, 16)
            act.wait_ge(o_out, 64 * PAIRS + 16)

        @block.tensor
        def _(pe):
            def transposes(dst, src):
                for e in range(2):
                    for h in range(HALVES):
                        ins = pe.transpose(dst[:, (e * HALVES + h) * P:(e * HALVES + h + 1) * P],
                                           src[:, e, h * P:(h + 1) * P], ident[:])
                return ins

            def adj_tile(u, v, e, l, first, last):
                w = adjT[:, u, e, :, v]
                t = 2 * u + v
                pe.matmul(accA[e][:, 0:D + 1], w, h1[l][:, t, 0:D + 1], start=first, stop=False)
                return pe.matmul(accA[e][:, 0:D], w, h2[l][:, t, :], start=False, stop=last)

            def unit(m, u):
                pe.wait_ge(e2_ok, m * PAIRS + (u + 1))
                for v in range(2):
                    t = 2 * u + v
                    for e in range(2):
                        zhi = Z[:, u, v, e * P:(e + 1) * P].bitcast(BF16).rearrange("p (i w) -> p i w", w=2)[:, :, 1]
                        zlo = E2[:, u, v, e * P:(e + 1) * P]
                        pe.matmul(accE[e][:, 0:D + 1], zhi, h1[0][:, t, 0:D + 1], start=(t == 0), stop=False)
                        pe.matmul(accE[e][:, 0:D], zhi, h2[0][:, t, :], start=False, stop=False)
                        ins = pe.matmul(accE[e][:, 0:D + 1], zlo, h1[0][:, t, 0:D + 1], start=False,
                                        stop=(t == TILES - 1))
                ins.then_inc(unit_done, 1)

            pe.wait_ge(consts, 6)
            for i in range(PAIRS + 5):
                if i < PAIRS:
                    pe.wait_ge(hf_ok[0], 2 * i + 2)
                    if i >= 2:
                        pe.wait_ge(hT_ok, i - 1)
                    dst = [tp, dA][i % 2]
                    for h in range(HALVES):
                        for e in range(2):
                            ins = pe.transpose(dst[:, (2 * h + e) * P:(2 * h + e + 1) * P],
                                               hf[:, i % 2, e, h * P:(h + 1) * P], ident[:])
                    ins.then_inc(hT_ps, 1)
                j = i - 1
                if 0 <= j < PAIRS:
                    if j == 0:
                        pe.wait_ge(wprep, 2 * HALVES)
                    pe.wait_ge(hT_ok, j + 1)
                    if j >= 1:
                        pe.wait_ge(sr99_ok, j)
                    for e in range(2):
                        for h in range(HALVES):
                            ins = pe.matmul(dB[0][:, 4 * e:4 * e + 4], hT[:, j % 2, h, e * P:(e + 1) * P],
                                            w4[:, h, :], start=(h == 0), stop=(h == HALVES - 1))
                    ins.then_inc(proj, 1)
                j = i - 2
                if 0 <= j < PAIRS:
                    pe.wait_ge(diag_ok, j + 1)
                    if j >= 1:
                        pe.wait_ge(sl_ok, j)
                    pe.matmul(dB[1][:, 0:2 * P], ones[:], diag[:].rearrange("p e n -> p (e n)"), start=True,
                              stop=True).then_inc(wide, 1)
                j = i - 2
                if 0 <= j < PAIRS:
                    if j == 0:
                        pe.wait_ge(tr_done, 1)
                    pe.wait_ge(h1_ok[0], j + 1)
                    pe.wait_ge(h2_ok, j + 1)
                    for v in range(2):
                        for e in range(2):
                            last = j == PAIRS - 1 and v == 1
                            ins = adj_tile(j, v, e, 0, j == 0 and v == 0, last)
                            if last:
                                ins.then_inc(a_done, 1)
                j = i - 5
                if 0 <= j < PAIRS:
                    unit(0, j)

            def adj_part(m, e):
                if e == 0:
                    pe.wait_ge(tr_done, m + 1)
                pe.wait_ge(th_ok, 2 * m + (e - 1))
                for u in range(PAIRS):
                    for v in range(2):
                        t = 2 * u + v
                        ins = adj_tile(u, v, e, 0, t == 0, t == TILES - 1)
                ins.then_inc(a_done, 1)

            def turn_a(m):
                pe.wait_ge(th_ok, 2 * m + 2)
                pe.wait_ge(tp_ev, 2 * m)
                transposes(tp, Th).then_inc(tp_w, 1)

            def dense_b(m):
                pe.wait_ge(tp_ev, 2 * m + 1)
                pe.wait_ge(ub_ok, 2 * m)
                for e in range(2):
                    for h in range(HALVES):
                        ins = pe.matmul(dB[e][:, 0:HW], TTa[:, e, h, :], wg[:, h, :], start=(h == 0),
                                        stop=(h == HALVES - 1))
                ins.then_inc(db_ok, 1)

            def turn_e(q):
                pe.wait_ge(ae_ok, 2 * q + 2)
                pe.wait_ge(tp_ev, 2 * q + 1)
                transposes(tp, AE).then_inc(tp_w, 1)

            def dense_a(q):
                pe.wait_ge(tp_ev, 2 * q + 2)
                pe.wait_ge(h2_ok, PAIRS + q)
                for e in range(2):
                    for h in range(HALVES):
                        ins = pe.matmul(dA[:, e * D:(e + 1) * D], TTe[:, e, h, :], wsa[:, h, :],
                                        start=(h == 0), stop=(h == HALVES - 1))
                ins.then_inc(da_ok, 1)

            def layer0(m, q):
                adj_part(m, 0)
                turn_e(q)
                adj_part(m, 1)
                dense_a(q)
                for u in range(PAIRS):
                    unit(m, u)
                    if u == 3:
                        turn_a(m)
                    if u == 8:
                        dense_b(m)

            pe.wait_ge(w2_in, 16 * N_W2DMA)
            turn_a(0)
            pe.wait_ge(sr99_ok, PAIRS)
            pe.wait_ge(sl_ok, PAIRS)
            dense_b(0)
            with pe.Fori(0, PAIRS - 1) as q:
                layer0(q + 1, q)

            def units(g, u0, u1):
                pe.wait_ge(h2_ok, PAIRS + u1)
                pe.wait_ge(h1_ok[1], u1)
                for u in range(u0, u1):
                    for v in range(2):
                        for e in range(2):
                            t = 2 * u + v
                            ins = adj_tile(u, v, e, 1, t == 0, t == TILES - 1)
                if u1 == AGROUPS[g][1]:
                    ins.then_inc(grp_done[g], 1)

            def group(m, g):
                pe.wait_ge(adj_ld[g], 16 * m + 16)
                units(g, *AGROUPS[g])

            def turn_p(q):
                pe.wait_ge(pool_ok, 2 * q + 2)
                transposes(tp, AE).then_inc(l1t_w, 1)

            def dense_p(q):
                pe.wait_ge(l1t_ev, q + 1)
                for e in range(2):
                    for h in range(HALVES):
                        ins = pe.matmul(dA[:, e * D:(e + 1) * D], TTa[:, e, h, :], w1[:, h, :],
                                        start=(h == 0), stop=(h == HALVES - 1))
                ins.then_inc(l1d_ok, 1)

            pe.wait_ge(th_ok, TILES)
            pe.wait_ge(adj_ld[0], 16)
            units(0, 0, 2)
            turn_e(PAIRS - 1)
            units(0, 2, 4)
            dense_a(PAIRS - 1)
            group(0, 1)
            pe.wait_ge(adj_ld[2], 16)
            units(2, 8, PAIRS - 1)
            units(2, PAIRS - 1, PAIRS)
            def layer1(q, first=False):
                pe.wait_ge(pool_ok, 2 * q + 2)
                group(q + 1, 0)
                turn_p(q)
                group(q + 1, 1)
                group(q + 1, 2)
                if not first:
                    pe.wait_ge(o_ok, q)
                dense_p(q)

            layer1(0, True)
            with pe.Fori(1, PAIRS - 1) as q:
                layer1(q)
            turn_p(PAIRS - 1)
            pe.wait_ge(o_ok, PAIRS - 1)
            dense_p(PAIRS - 1)

        @block.vector
        def _(dve):
            dve.memset(stage[96:P, :, :, QN - 1:QN], 0.0).then_inc(pads, 1)
            dve.memset(xs[96:P, TILES - 1, :], 0.0).then_inc(pads, 1)
            dve.memset(bias4[:, :, 0:1], 0.0)
            dve.memset(bias4[:, :, 3:4], 0.0).then_inc(wchain, 1)

            def pair_stats(i, slot, par, l, src):
                if l:
                    dve.wait_ge(nmr_ok[0], PAIRS)
                    dve.wait_ge(x1_ok, i + 1)
                for e in range(2):
                    ins = dve.bn_stats(bst[:, par, e], src[:, e])
                ins.then_inc(bnr[l], 1)
                if l:
                    dve.wait_ge(nmr_ok[0], PAIRS)
                dve.wait_ge(bnr[l], i + 1)
                for e in range(2):
                    ins = dve.bn_aggr(mv[:, slot, e], bst[:, par, e])
                ins.then_inc(stats[l], 1)

            def pair_nmr(i, par, l):
                dve.wait_ge(rstd_ok[l], i + 1)
                dve.scalar_tensor_tensor(out=nmr[:, par], in0=mv[:, par, :, 0], scalar=-1.0, in1=rstd[:, par],
                                         op0=ALU.mult, op1=ALU.mult).then_inc(nmr_ok[l], 1)

            def second_part(i, par, l, first, dst):
                dve.wait_ge(h1_ok[l], i + 1)
                dve.tensor_tensor(dst, hf[:, par], first, ALU.subtract).then_inc(h2_ok, 1)

            def turn_adj():
                for e in range(2):
                    src = stage[:, e].bitcast(U32).rearrange("p b (u r) -> p b u r", r=QUAD)
                    dst = adjT[:, :, e].rearrange("p u (b c) v -> p b u (c v)", b=4).bitcast(U32)
                    ins = dve.transpose(dst, src)
                ins.then_inc(tr_done, 1)

            def weights():
                dve.wait_ge(w_in, 16 * N_WDMA)
                for h in range(HALVES):
                    for k, dst in enumerate((w4[:, h, 3:4], w4[:, h, 0:1])):
                        dve.tensor_tensor_reduce(out=prod[:, 2 * h + k], in0=wsa[:, h, :], in1=arep[:, k * D:(k + 1) * D],
                                                 scale=1.0, scalar=0.0, op0=ALU.mult, op1=ALU.add,
                                                 accum_out=dst).then_inc(wprep, 1)

            def mask(m, u):
                dve.wait_ge(exp_ok, m * PAIRS + (u + 1))
                for v in range(2):
                    t = 2 * u + v
                    ins = dve.scalar_tensor_tensor(out=Z[:, u, v], in0=adjT[:, u, :, :, v].rearrange("p e i -> p (e i)"),
                                                   scalar=vr[:, t:t + 1], in1=Z[:, u, v], op0=ALU.mult, op1=ALU.mult)
                ins.then_inc(mask_ok, 1)

            def split(m, u):
                dve.wait_ge(mask_ok, m * PAIRS + (u + 1))
                hi = Z[:, u].bitcast(BF16).rearrange("p v (i w) -> p v i w", w=2)[:, :, :, 1]
                dve.tensor_tensor(E2[:, u], Z[:, u], hi, ALU.subtract).then_inc(e2_ok, 1)

            def first_stats(i):
                g = [g for g, (a, b) in enumerate(GROUPS) if a <= i < b][0]
                dve.wait_ge(x_in[g], 16 * (4 if g < len(GROUPS) - 1 else 6))
                if i >= 2:
                    dve.wait_ge(stats[0], i - 1)
                pair_stats(i, i, i % 2, 0, xs[:, 2 * i:2 * i + 2])

            first_stats(0)
            first_stats(1)
            weights()
            pair_nmr(0, 0, 0)
            for i in range(PAIRS + 4):
                if i + 2 < PAIRS:
                    first_stats(i + 2)
                if i + 1 < PAIRS:
                    pair_nmr(i + 1, i + 1, 0)
                j = i - 2
                if 0 <= j < PAIRS:
                    dve.wait_ge(proj, j + 1)
                    if j == 0:
                        dve.wait_ge(wchain, 1)
                    taken = dB[0][:, 0:8].rearrange("p (e k) -> p e k", k=4)
                    dve.tensor_tensor(srw[:, 2 * j:2 * j + 2, :], taken, bias4[:], ALU.add).then_inc(srw_ok, 1)
                    dve.tensor_scalar(sr99[:, 2 * j:2 * j + 2], taken[:, :, 0], 1.0 - SLOPE, None,
                                      ALU.mult).then_inc(sr99_ok, 1)
                    dve.wait_ge(srw_ok, j + 1)
                    if j >= 1:
                        dve.wait_ge(wide, j)
                    for e in range(2):
                        ins = dve.tensor_scalar(diag[:, e], ident[:], srw[:, 2 * j + e, 3:4], None, ALU.mult)
                    ins.then_inc(diag_ok, 1)
                j = i - 1
                if 0 <= j < PAIRS:
                    second_part(j, j % 2, 0, h1[0][:, 2 * j:2 * j + 2, 0:D], h2[0][:, 2 * j:2 * j + 2])
                if i == 1:
                    dve.wait_ge(adj_in, 16 * 8)
                    turn_adj()
                    dve.wait_ge(tr_done, 1)
                j = i - 4
                if 0 <= j < PAIRS:
                    dve.wait_ge(vr_ok, j + 1)
                    mask(0, j)
                    split(0, j)

            def degrees(m):
                dve.wait_ge(th_ok, 2 * m + 2)
                dve.tensor_scalar(degm[:], Th[:, :, ones_col], 1.0, None, ALU.max).then_inc(deg_c, 1)
                dve.wait_ge(deg_c, m + 1)
                dve.reciprocal(dr[:, bass.ds(2 * m, 2)], degm[:]).then_inc(deg_ok, 1)

            def row_sums(q):
                dve.wait_ge(unit_done, q * PAIRS + PAIRS)
                for e in range(2):
                    ins = dve.scalar_tensor_tensor(out=ssum[:, e:e + 1], in0=el[:, bass.ds(2 * q + e, 1)],
                                                   scalar=SUM_EPS, in1=accE[e][:, ones_col:ones_col + 1],
                                                   op0=ALU.mult, op1=ALU.add)
                ins.then_inc(rs_c, 1)
                dve.wait_ge(rs_c, q + 1)
                dve.reciprocal(rs[:], ssum[:]).then_inc(rs_ok, 1)

            def gate_args(q):
                dve.wait_ge(db_ok, q + 1)
                for e in range(2):
                    ins = dve.tensor_tensor(zg[:, e:e + 1], dB[e][:, D:HW].rearrange("p (a k) -> p a k", a=1),
                                            srw[:, bass.ds(2 * q + e, 1), 1:3], ALU.add)
                ins.then_inc(zg_ok, 1)

            def gates(q):
                dve.wait_ge(eg_ok, q + 1)
                dve.tensor_scalar(eg1[:], eg[:], 1.0, None, ALU.add).then_inc(gate_c, 1)
                dve.wait_ge(gate_c, q + 1)
                dve.reciprocal(gate[:], eg1[:]).then_inc(gate_ok, 1)

            def mix(q):
                dve.wait_ge(ub_ok, 2 * q + 2)
                dve.wait_ge(w2_in, 16 * N_W2DMA)
                for e in range(2):
                    dve.scalar_tensor_tensor(out=wm[:, e], in0=bgrep[:], scalar=gate[:, e, 1:2], in1=ub[:, e],
                                             op0=ALU.mult, op1=ALU.add).then_inc(wm_c, 1)
                dve.wait_ge(da_ok, q + 1)
                for e in range(2):
                    dve.wait_ge(wm_c, 2 * q + (e + 1))
                    dve.scalar_tensor_tensor(out=wm[:, e], in0=dA[:, e * D:(e + 1) * D],
                                             scalar=gate[:, e, 0:1], in1=wm[:, e], op0=ALU.mult,
                                             op1=ALU.add).then_inc(wm_ok, 1)

            def residual(q):
                dve.wait_ge(h2_ok, PAIRS + q)
                dve.wait_ge(wx_ok, q + 1)
                dve.tensor_scalar(wm[:], wx[:], 0.5, 0.5, ALU.mult, ALU.add).then_inc(x1_c, 1)
                dve.wait_ge(x1_c, q + 1)
                dve.tensor_tensor(xs[:, bass.ds(2 * q, 2)], xs[:, bass.ds(2 * q, 2)], wm[:],
                                  ALU.add).then_inc(x1_ok, 1)
                pair_stats(q, 0, 0, 1, xs[:, bass.ds(2 * q, 2)])

            def later_second(q):
                second_part(q, 0, 1, h1[1][:, bass.ds(2 * q, 2), 0:D], h2[1][:, bass.ds(2 * q, 2)])

            def next_adj(m, adj_count):
                dve.wait_ge(adj_in, adj_count)
                dve.wait_ge(a_done, 2 * m)
                dve.wait_ge(stored, 16 * m)
                dve.wait_ge(mask_ok, m * PAIRS)
                turn_adj()

            def layer0(m, q, p, adj_count):
                dve.wait_ge(tr_done, m + 1)
                for u in range(PAIRS + 1):
                    if u < PAIRS:
                        mask(m, u)
                    if u >= 1:
                        split(m, u - 1)
                    if p is not None:
                        if u == 1:
                            pair_nmr(p, 0, 1)
                        if u == 9:
                            later_second(p)
                    if u == 9:
                        row_sums(q)
                        gate_args(q)
                    if u == 11:
                        gates(q)
                mix(q)
                degrees(m)
                if adj_count is not None:
                    next_adj(m + 1, adj_count)
                residual(q)

            next_adj(1, 128 * 2)
            degrees(0)
            dve.wait_ge(vr_ok, PAIRS + 1)
            layer0(1, 0, None, 128 * 3)
            with dve.Fori(0, PAIRS - 4) as q:
                layer0(q + 2, q + 1, q, q * 128 + 512)
            last = PAIRS - 1
            layer0(last - 1, last - 2, last - 3, 128 * PAIRS + 64)
            layer0(last, last - 1, last - 2, None)
            pair_nmr(last - 1, 0, 1)
            row_sums(last)
            gate_args(last)
            later_second(last - 1)
            gates(last)
            mix(last)
            residual(last)
            pair_nmr(last, 0, 1)
            later_second(last)

            def pooled(m):
                dve.wait_ge(grp_done[-1], m + 1)
                dve.wait_ge(hp_ok, m + 1)
                dve.tensor_copy(drp[:], dr[:, bass.ds(2 * m, 2)]).then_inc(drp_ok, 1)
                for e in range(2):
                    dve.tensor_tensor(wm[:, e], accA[e][:, 0:D], hp[:, e], ALU.add).then_inc(pt_c, 1)
                dve.wait_ge(drp_ok, m + 1)
                for e in range(2):
                    dve.wait_ge(pt_c, 2 * m + (e + 1))
                    dve.scalar_tensor_tensor(out=AE[:, e], in0=wm[:, e], scalar=drp[:, e:e + 1], in1=hp[:, e],
                                             op0=ALU.mult, op1=ALU.add).then_inc(pool_ok, 1)

            def output(q, first=False):
                dve.wait_ge(l1d_ok, q + 1)
                dve.tensor_tensor(wx[:], dA[:].rearrange("p (e d) -> p e d", e=2),
                                  bass.AP(b1rep[:].tensor, 0, [[D, P], [0, 2], [1, D]]), ALU.add).then_inc(ob_c, 1)
                dve.wait_ge(ob_c, q + 1)
                if not first:
                    dve.wait_ge(o_out, 64 * q)
                dve.scalar_tensor_tensor(out=osb[:], in0=wx[:], scalar=0.0, in1=xs[:, bass.ds(2 * q, 2)],
                                         op0=ALU.max, op1=ALU.add).then_inc(o_ok, 1)

            pooled(0)
            dve.wait_ge(l1t_w, 1)
            pooled(1)
            output(0, True)
            with dve.Fori(1, PAIRS - 1) as q:
                dve.wait_ge(l1t_w, q + 1)
                pooled(q + 1)
                output(q)
            output(PAIRS - 1)


_INS = ['x', 'adj', 'L0_gnn_W_sa', 'L0_gnn_a_sa', 'L0_gnn_W_gcnb', 'L0_gnn_b_gcnb', 'L0_gnn_Wa', 'L0_gnn_ba',
        'L0_gnn_Wb', 'L0_gnn_bb', 'L1_gnn_W', 'L1_gnn_b']


def kernel(**inputs):
    import numpy as _np
    import concourse.bacc as _bacc
    from concourse import mybir as _mybir
    from concourse.bass_utils import run_bass_kernel_spmd as _run

    nc = _bacc.Bacc("TRN2", target_bir_lowering=False, num_devices=1)
    arrays, args = {}, []
    for name in _INS:
        a = _np.ascontiguousarray(inputs[name])
        arrays[f"in_{name}_dram"] = a
        args.append(nc.dram_tensor(f"in_{name}_dram", a.shape, _mybir.dt.from_np(a.dtype), kind="ExternalInput").ap())
    shape = inputs['x'].shape
    args.append(nc.dram_tensor("out_0_dram", shape, _mybir.dt.float32, kind="ExternalOutput").ap())
    gnn_kernel(nc, *args)
    r = _run(nc, [arrays], core_ids=[0])
    return r.results[0]["out_0_dram"]
```

```python
from contextlib import ExitStack

import concourse.bass as bass
from concourse import mybir

F32 = mybir.dt.float32
F16 = mybir.dt.float16
BF16 = mybir.dt.bfloat16
U32 = mybir.dt.uint32
ALU = mybir.AluOpType
ACT = mybir.ActivationFunctionType

P = 128
QUAD = 32
LN_EPS = 1e-5
SUM_EPS = 1e-5
SLOPE = 0.01


def gnn_kernel(nc, x, adj, W_sa, a_sa, W_g, b_g, Wa, ba, Wb, bb, W1, b1, out):
    N, D = x.shape
    PAIRS = -(-N // (2 * P))
    TILES = 2 * PAIRS
    QN = TILES * QUAD
    HALVES = D // P
    HW = D + 2
    ones_col = D
    GROUPS = [(0, 2), (2, 4), (4, 8), (8, PAIRS)]
    TURNS = [(0, 4), (4, 9), (9, PAIRS)]
    BATCHES = [(0, 1), (1, 2), (2, 4), (4, 8), (8, PAIRS)]
    AGROUPS = [(0, 4), (4, 8), (8, PAIRS)]

    with ExitStack() as ctx:
        def sb(name, shape, dt=F32):
            return ctx.enter_context(nc.sbuf_tensor(name, shape, dt))

        def ps(name):
            return ctx.enter_context(nc.psum_tensor(name, [P, 512], F32))

        def sem(name):
            return ctx.enter_context(nc.semaphore(name))

        adjT_store = nc.dram_tensor("adjT_store", [PAIRS, P, PAIRS * 256], U32, kind="Internal").ap()

        xs = sb("xs", [P, TILES, D])
        h1 = [sb(f"h1_{l}", [P, TILES, HW], F16) for l in range(2)]
        h2 = [sb(f"h2_{l}", [P, TILES, D], F16) for l in range(2)]
        stage = sb("stage", [P, 2, 4, QN], BF16)
        adjT = sb("adjT", [P, PAIRS, 2, P, 2], BF16)
        Z = sb("Z", [P, PAIRS, 2, 2 * P])
        E2 = sb("E2", [P, PAIRS, 2, 2 * P], BF16)
        sl = sb("sl", [P, TILES * P])
        slp = sb("slp", [P, 2 * P])
        srw = sb("srw", [P, TILES, 4])
        sr99 = sb("sr99", [P, TILES])
        vr = sb("vr", [P, TILES])
        el = sb("el", [P, TILES])
        bst = sb("bst", [P, 2, 2, 6])
        mv = sb("mv", [P, PAIRS, 2, 2])
        ve = sb("ve", [P, PAIRS, 2])
        rstd = sb("rstd", [P, PAIRS, 2])
        nmr = sb("nmr", [P, PAIRS, 2])
        halfs = sb("halfs", [P, PAIRS, 2])
        epss = sb("epss", [P, PAIRS, 2])
        hf = sb("hf", [P, 2, 2, D])
        hT = sb("hT", [P, 2, HALVES, 2 * P])
        ident = sb("ident", [P, P])
        wsa = sb("wsa", [P, HALVES, D])
        wg = sb("wg", [P, HALVES, HW])
        w1 = sb("w1", [P, HALVES, D])
        w4 = sb("w4", [P, HALVES, 4])
        diag = sb("diag", [P, 2, P])
        ones = sb("ones", [P, P])
        arep = sb("arep", [P, 2 * D])
        prod = sb("prod", [P, 2 * HALVES, D])
        bias4 = sb("bias4", [P, 2, 4])
        bgrep = sb("bgrep", [P, D])
        b1rep = sb("b1rep", [P, D])
        Th = sb("Th", [P, 2, HW])
        AE = sb("AE", [P, 2, D])
        TTa = sb("TTa", [P, 2, HALVES, P])
        TTe = sb("TTe", [P, 2, HALVES, P])
        degm = sb("degm", [P, 2])
        dr = sb("dr", [P, TILES])
        drp = sb("drp", [P, 2])
        ssum = sb("ssum", [P, 2])
        rs = sb("rs", [P, 2])
        zg = sb("zg", [P, 2, 2])
        eg = sb("eg", [P, 2, 2])
        eg1 = sb("eg1", [P, 2, 2])
        gate = sb("gate", [P, 2, 2])
        ub = sb("ub", [P, 2, D])
        wm = sb("wm", [P, 2, D])
        wx = sb("wx", [P, 2, D])
        hp = sb("hp", [P, 2, D])
        osb = sb("osb", [P, 2, D])

        accE = [ps("accE0"), ps("accE1")]
        accA = [ps("accA0"), ps("accA1")]
        tp = ps("tp")
        dB = [ps("dB0"), ps("dB1")]
        dA = ps("dA")

        x_in = [sem(f"x_in{g}") for g in range(len(GROUPS))]
        w_in = sem("w_in")
        bias_in = sem("bias_in")
        w2_in = sem("w2_in")
        pads = sem("pads")
        consts = sem("consts")
        id0 = sem("id0")
        wprep = sem("wprep")
        wchain = sem("wchain")
        stats = [sem(f"stats_{l}") for l in range(2)]
        bnr = [sem(f"bnr_{l}") for l in range(2)]
        vplus = [sem(f"vplus_{l}") for l in range(2)]
        rstd_ok = [sem(f"rstd_ok_{l}") for l in range(2)]
        nmr_ok = [sem(f"nmr_ok_{l}") for l in range(2)]
        hf_ok = [sem(f"hf_ok_{l}") for l in range(2)]
        h1_ok = [sem(f"h1_ok_{l}") for l in range(2)]
        h2_ok = sem("h2_ok")
        hT_ps = sem("hT_ps")
        hT_ok = sem("hT_ok")
        proj = sem("proj")
        diag_ok = sem("diag_ok")
        wide = sem("wide")
        srw_ok = sem("srw_ok")
        sl_ok = sem("sl_ok")
        adj_in = sem("adj_in")
        tr_done = sem("tr_done")
        tr_part = sem("tr_part")
        stored = sem("stored")
        a_done = sem("a_done")
        slp_ok = sem("slp_ok")
        vr_ok = sem("vr_ok")
        sr99_ok = sem("sr99_ok")
        pl_ok = sem("pl_ok")
        exp_ok = sem("exp_ok")
        mask_ok = sem("mask_ok")
        e2_ok = sem("e2_ok")
        unit_done = sem("unit_done")
        th_ok = sem("th_ok")
        deg_c = sem("deg_c")
        deg_ok = sem("deg_ok")
        tp_w = sem("tp_w")
        tp_ev = sem("tp_ev")
        db_ok = sem("db_ok")
        da_ok = sem("da_ok")
        rs_c = sem("rs_c")
        rs_ok = sem("rs_ok")
        ae_ok = sem("ae_ok")
        zg_ok = sem("zg_ok")
        eg_ok = sem("eg_ok")
        gate_c = sem("gate_c")
        gate_ok = sem("gate_ok")
        ub_ok = sem("ub_ok")
        wm_c = sem("wm_c")
        wm_ok = sem("wm_ok")
        wx_ok = sem("wx_ok")
        x1_c = sem("x1_c")
        x1_ok = sem("x1_ok")
        adj_ld = [sem(f"adj_ld{g}") for g in range(len(AGROUPS))]
        grp_done = [sem(f"grp_done{g}") for g in range(len(AGROUPS))]
        hp_ok = sem("hp_ok")
        pt_c = sem("pt_c")
        pool_ok = sem("pool_ok")
        drp_ok = sem("drp_ok")
        l1t_w = sem("l1t_w")
        l1t_ev = sem("l1t_ev")
        l1d_ok = sem("l1d_ok")
        ob_c = sem("ob_c")
        o_ok = sem("o_ok")
        o_out = sem("o_out")

        N_WDMA = 4
        N_W2DMA = 6

        def load_x(engine, g, quadrants=range(4)):
            u0, u1 = GROUPS[g]
            for b in quadrants:
                full = u1 if (b < 3 or u1 < PAIRS) else PAIRS - 1
                src = bass.AP(x.tensor, (QN * b + 64 * u0) * D, [[2 * D, QUAD], [64 * D, full - u0], [1, 2 * D]])
                dst = xs[32 * b:32 * b + 32, 2 * u0:2 * full, :].rearrange("p (u v) d -> p u (v d)", v=2)
                engine.dma_start(dst, src).then_inc(x_in[g], 16)
                if full < u1:
                    r0 = QN * b + 64 * full
                    src = bass.AP(x.tensor, r0 * D, [[2 * D, QUAD - 1], [1, 2 * D]])
                    dst = xs[96:96 + QUAD - 1, 2 * full:2 * u1, :].rearrange("p v d -> p (v d)")
                    engine.dma_start(dst, src).then_inc(x_in[g], 16)
                    src = bass.AP(x.tensor, (N - 1) * D, [[D, 1], [1, D]])
                    engine.dma_start(xs[P - 1:P, 2 * full, :], src).then_inc(x_in[g], 16)

        def batch_of(i):
            return [n for n, (a, b) in enumerate(BATCHES) if a <= i < b][0]

        block = ctx.enter_context(nc.Block())

        @block.sync
        def _(sp):
            load_x(sp, 0, (0, 1))
            sp.wait_ge(pads, 2)
            for g in range(1, len(GROUPS)):
                load_x(sp, g)
                if g == 1:
                    sp.wait_ge(w_in, 16 * N_WDMA)
            sp.dma_start(wg[:, :, 0:D], W_g.rearrange("(h p) o -> p h o", p=P)).then_inc(w2_in, 16)
            sp.dma_start(bgrep[:], bass.AP(b_g.tensor, 0, [[0, P], [1, D]])).then_inc(w2_in, 16)
            sp.dma_start(w1[:], W1.rearrange("(h p) o -> p h o", p=P)).then_inc(w2_in, 16)
            sp.dma_start(b1rep[:], bass.AP(b1.tensor, 0, [[0, P], [1, D]])).then_inc(w2_in, 16)
            with sp.Fori(0, PAIRS) as q:
                sp.wait_ge(tr_done, q + 1)
                sp.dma_start(adjT_store[bass.ds(q, 1)].rearrange("a p n -> p (a n)"),
                             adjT[:].rearrange("p u e i v -> p (u e i v)").bitcast(U32)).then_inc(stored, 16)
            sp.wait_ge(stored, 16 * PAIRS)

            def load_pair(q):
                for g, (u0, u1) in enumerate(AGROUPS):
                    yield g, (adjT[:, u0:u1].rearrange("p u e i v -> p (u e i v)").bitcast(U32),
                              adjT_store[bass.ds(q, 1), :, 256 * u0:256 * u1].rearrange("a p n -> p (a n)"))

            sp.wait_ge(mask_ok, PAIRS * PAIRS)
            sp.wait_ge(a_done, TILES)
            for g, (dst, src) in load_pair(0):
                sp.dma_start(dst, src).then_inc(adj_ld[g], 16)

            with sp.Fori(0, PAIRS - 1) as q:
                for g, (dst, src) in load_pair(q + 1):
                    sp.wait_ge(grp_done[g], q + 1)
                    sp.dma_start(dst, src).then_inc(adj_ld[g], 16)

        @block.gpsimd
        def _(pool):
            pool.memset(ident[:], 0.0).then_inc(id0, 1)
            pool.memset(ones[:], 1.0).then_inc(consts, 1)
            pool.memset(halfs[:], -0.5).then_inc(consts, 1)
            pool.memset(epss[:], LN_EPS).then_inc(consts, 1)
            for l in range(2):
                pool.memset(h1[l][:, :, ones_col:HW], 1.0).then_inc(consts, 1)
            pool.wait_ge(id0, 1)
            pool.affine_select(out=ident[:], in_=ident[:], compare_op=ALU.not_equal, fill=1.0, base=0,
                               pattern=[[-1, P]], channel_multiplier=1).then_inc(consts, 1)

            def load_adj(q, quadrants=range(4)):
                for b in quadrants:
                    w = QN if b < 3 else QN - 1
                    src = bass.AP(adj.tensor, q * (64 * N) + QN * b, [[2 * N, QUAD], [N, 2], [QN * N, 4], [1, w]])
                    pool.dma_start(stage[32 * b:32 * b + 32, :, :, 0:w], src).then_inc(adj_in, 16)

            def load_last_adj():
                for b in range(4):
                    w = QN if b < 3 else QN - 1
                    base = (PAIRS - 1) * 64 * N + QN * b
                    for e, r0, r1, rows in ((0, 0, 4, QUAD), (1, 0, 3, QUAD), (1, 3, 4, QUAD - 1)):
                        src = bass.AP(adj.tensor, base + (e + r0 * QN) * N,
                                      [[2 * N, rows], [QN * N, r1 - r0], [1, w]])
                        pool.dma_start(stage[32 * b:32 * b + rows, e, r0:r1, 0:w], src).then_inc(adj_in, 16)

            def inv_std(q):
                pool.wait_ge(stats[1], q + 1)
                pool.tensor_tensor(ve[:, 0], mv[:, 0, :, 1], epss[:, 0], ALU.add).then_inc(vplus[1], 1)
                pool.wait_ge(vplus[1], q + 1)
                pool.wait_ge(h2_ok, PAIRS + q)
                pool.tensor_tensor(rstd[:, 0], ve[:, 0], halfs[:, 0], ALU.pow).then_inc(rstd_ok[1], 1)

            def inv_stds(n):
                a, b = BATCHES[n]
                pool.wait_ge(stats[0], b)
                pool.tensor_tensor(ve[:, a:b], mv[:, a:b, :, 1], epss[:, 0:b - a], ALU.add).then_inc(vplus[0], 1)
                pool.wait_ge(vplus[0], n + 1)
                pool.tensor_tensor(rstd[:, a:b], ve[:, a:b], halfs[:, 0:b - a], ALU.pow).then_inc(rstd_ok[0], 1)

            def first_part(i, par, l, dst):
                pool.wait_ge(hf_ok[l], 2 * i + 2)
                pool.tensor_copy(dst, hf[:, par]).then_inc(h1_ok[l], 1)

            def later_first(q):
                first_part(q, 0, 1, h1[1][:, bass.ds(2 * q, 2), 0:D])

            pool.wait_ge(pads, 1)
            load_adj(0)
            pool.wait_ge(consts, 6)
            inv_stds(0)
            inv_stds(1)
            for i in range(PAIRS):
                first_part(i, i % 2, 0, h1[0][:, 2 * i:2 * i + 2, 0:D])
                if i in (0, 2, 5):
                    inv_stds({0: 2, 2: 3, 5: 4}[i])
                if 3 <= i < 7:
                    pool.wait_ge(tr_done, 1)
                    load_adj(1, quadrants=(i - 3,))

            pool.wait_ge(tr_done, 2)
            load_adj(2)
            with pool.Fori(0, PAIRS - 4) as q:
                inv_std(q)
                pool.wait_ge(tr_done, q + 3)
                load_adj(q + 3)
                later_first(q)
            inv_std(PAIRS - 4)
            pool.wait_ge(tr_done, PAIRS - 1)
            pool.memset(stage[:, 1, 3, :], 0.0).then_inc(pads, 1)
            pool.wait_ge(pads, 3)
            load_last_adj()
            later_first(PAIRS - 4)
            for q in range(PAIRS - 3, PAIRS):
                inv_std(q)
                later_first(q)

            def self_h(q):
                pool.tensor_tensor(hp[:], h1[1][:, bass.ds(2 * q, 2), 0:D], h2[1][:, bass.ds(2 * q, 2), :],
                                   ALU.add).then_inc(hp_ok, 1)
            pool.wait_ge(h2_ok, 2 * PAIRS)
            self_h(0)
            with pool.Fori(0, PAIRS - 1) as q:
                pool.wait_ge(pool_ok, 2 * q + 2)
                self_h(q + 1)

        @block.scalar
        def _(act):
            def wdma(dst, src, scattered=False):
                act.dma_start(dst, src, allow_slow_non_contiguous=scattered).then_inc(w_in, 16)

            load_x(act, 0, (2, 3))
            rep = lambda t, off, n: bass.AP(t.tensor, off, [[0, P], [1, n]])
            for k, w in enumerate((Wa, Wb)):
                wdma(w4[:, :, 1 + k], w[0, D:2 * D].rearrange("(h p) -> p h", p=P), True)
            wdma(wsa[:], W_sa.rearrange("(h p) o -> p h o", p=P))
            wdma(arep[:], rep(a_sa, 0, 2 * D))
            for e in range(2):
                act.dma_start(bias4[:, e, 1:2], rep(ba, 0, 1)).then_inc(bias_in, 16)
                act.dma_start(bias4[:, e, 2:3], rep(bb, 0, 1)).then_inc(bias_in, 16)
            for k, w in enumerate((Wa, Wb)):
                act.dma_start(wg[:, :, D + k], w[0, 0:D].rearrange("(h p) -> p h", p=P),
                              allow_slow_non_contiguous=True).then_inc(w2_in, 16)

            def norm(i, slot, par, l, src):
                if l:
                    act.wait_ge(hT_ps, PAIRS)
                act.wait_ge(nmr_ok[l], i + 1 if l else batch_of(i) + 1)
                for e in range(2):
                    act.activation(hf[:, par, e], src[:, e], ACT.Relu, bias=nmr[:, slot, e:e + 1],
                                   scale=rstd[:, slot, e:e + 1]).then_inc(hf_ok[l], 1)

            def leaky(m, u, fresh):
                if not fresh:
                    act.wait_ge(unit_done, (m - 1) * PAIRS + (u + 1))
                for v in range(2):
                    t = 2 * u + v
                    ins = act.activation(Z[:, u, v], slp[:], ACT.Relu, bias=sr99[:, t:t + 1], scale=1.0 - SLOPE)
                ins.then_inc(pl_ok, 1)

            def expo(m, u):
                act.wait_ge(pl_ok, m * PAIRS + (u + 1))
                act.activation(Z[:, u], Z[:, u], ACT.Exp, scale=-1.0).then_inc(exp_ok, 1)

            for i in range(PAIRS + 4):
                if i < PAIRS:
                    act.wait_ge(x_in[[g for g, (a, b) in enumerate(GROUPS) if a <= i < b][0]],
                                16 * (4 if i < GROUPS[-1][0] else 6))
                    if i >= 2:
                        act.wait_ge(h2_ok, i - 1)
                        act.wait_ge(hT_ps, i - 1)
                    norm(i, i, i % 2, 0, xs[:, 2 * i:2 * i + 2])
                j = i - 1
                if 0 <= j < PAIRS:
                    act.wait_ge(hT_ps, j + 1)
                    if j >= 2:
                        act.wait_ge(proj, j - 1)
                    act.activation(hT[:, j % 2], [tp, dA][j % 2][:].rearrange("p (h n) -> p h n", h=HALVES),
                                   ACT.Copy).then_inc(hT_ok, 1)
                j = i - 3
                if 0 <= j < PAIRS:
                    act.wait_ge(srw_ok, j + 1)
                    act.activation(vr[:, 2 * j:2 * j + 2], srw[:, 2 * j:2 * j + 2, 0], ACT.Exp,
                                   scale=-SLOPE).then_inc(vr_ok, 1)
                    act.wait_ge(wide, j + 1)
                    act.activation(sl[:, 2 * P * j:2 * P * (j + 1)], dB[1][:, 0:2 * P],
                                   ACT.Copy).then_inc(sl_ok, 1)
                    if j == 0:
                        act.wait_ge(sl_ok, 1)
                        act.activation(slp[:], sl[:, 0:2 * P], ACT.Copy).then_inc(slp_ok, 1)
                        act.wait_ge(slp_ok, 1)
                    act.wait_ge(sr99_ok, j + 1)
                    leaky(0, j, True)
                j = i - 4
                if 0 <= j < PAIRS:
                    expo(0, j)
            act.wait_ge(sl_ok, PAIRS)


            def sums_out(m, e):
                act.wait_ge(a_done, 2 * m + (e + 1))
                if e == 0:
                    act.wait_ge(deg_ok, m)
                    act.wait_ge(tp_w, 2 * m)
                act.activation(Th[:, e, 0:D + 1], accA[e][:, 0:D + 1], ACT.Copy).then_inc(th_ok, 1)

            def turned_a(m):
                act.wait_ge(tp_w, 2 * m + 1)
                act.wait_ge(db_ok, m)
                act.activation(TTa[:].rearrange("p e h i -> p (e h i)"), tp[:], ACT.Copy).then_inc(tp_ev, 1)

            def attn_out(q):
                act.wait_ge(rs_ok, q + 1)
                for e in range(2):
                    act.activation(AE[:, e], accE[e][:, 0:D], ACT.Copy, scale=rs[:, e:e + 1]).then_inc(ae_ok, 1)

            def turned_e(q):
                act.wait_ge(tp_w, 2 * q + 2)
                act.activation(TTe[:].rearrange("p e h i -> p (e h i)"), tp[:], ACT.Copy).then_inc(tp_ev, 1)

            def gate_exp(q):
                act.wait_ge(zg_ok, q + 1)
                act.activation(eg[:], zg[:], ACT.Exp, scale=-1.0).then_inc(eg_ok, 1)

            def gated_b(q):
                act.wait_ge(gate_ok, q + 1)
                act.wait_ge(db_ok, q + 1)
                for e in range(2):
                    act.activation(ub[:, e], dB[e][:, 0:D], ACT.Copy, scale=gate[:, e, 1:2]).then_inc(ub_ok, 1)

            def half_tanh(q):
                act.wait_ge(wm_ok, 2 * q + 2)
                act.activation(wx[:], wm[:], ACT.Tanh, scale=0.5).then_inc(wx_ok, 1)

            def norm_later(q):
                act.wait_ge(x1_ok, q + 1)
                act.wait_ge(h2_ok, PAIRS + q)
                norm(q, 0, 0, 1, xs[:, bass.ds(2 * q, 2)])

            def layer0(m, q, p, sums_at=10, turn_at=PAIRS):
                act.activation(slp[:], sl[:, bass.ds(m * (2 * P), 2 * P)], ACT.Copy).then_inc(slp_ok, 1)
                act.wait_ge(slp_ok, m + 1)
                for u in range(PAIRS + 1):
                    if u < PAIRS:
                        leaky(m, u, False)
                    if u >= 1:
                        expo(m, u - 1)
                    if p is not None and u == 3:
                        norm_later(p)
                    if u == sums_at:
                        attn_out(q)
                        gate_exp(q)
                    if u == turn_at:
                        gated_b(q)
                        sums_out(m, 0)
                        turned_e(q)
                sums_out(m, 1)
                half_tanh(q)
                turned_a(m)

            sums_out(0, 0)
            sums_out(0, 1)
            act.activation(el[:], srw[:, :, 3], ACT.Exp, scale=SLOPE).then_inc(vr_ok, 1)
            turned_a(0)
            layer0(1, 0, None, 1, 6)
            with act.Fori(0, PAIRS - 2) as q:
                layer0(q + 2, q + 1, q)
            last = PAIRS - 1
            norm_later(last - 1)
            attn_out(last)
            gate_exp(last)
            gated_b(last)
            turned_e(last)
            half_tanh(last)
            norm_later(last)

            def turned_p(q):
                act.wait_ge(l1t_w, q + 1)
                act.activation(TTa[:].rearrange("p e h i -> p (e h i)"), tp[:], ACT.Copy).then_inc(l1t_ev, 1)
            def store_out(q, rows=QUAD):
                for b in range(4):
                    k = rows if b == 3 else QUAD
                    dst = bass.AP(out.tensor, (QN * b) * D + q * (64 * D), [[2 * D, k], [1, 2 * D]])
                    act.dma_start(dst, osb[32 * b:32 * b + k].rearrange("p e d -> p (e d)")).then_inc(o_out, 16)

            turned_p(0)
            with act.Fori(0, PAIRS - 1) as q:
                act.wait_ge(o_ok, q + 1)
                store_out(q)
                turned_p(q + 1)
            act.wait_ge(o_ok, PAIRS)
            store_out(PAIRS - 1, QUAD - 1)
            dst = bass.AP(out.tensor, (N - 1) * D, [[D, 1], [1, D]])
            act.dma_start(dst, osb[P - 1:P, 0, :]).then_inc(o_out, 16)
            act.wait_ge(o_out, 64 * PAIRS + 16)

        @block.tensor
        def _(pe):
            def transposes(dst, src):
                for e in range(2):
                    for h in range(HALVES):
                        ins = pe.transpose(dst[:, (e * HALVES + h) * P:(e * HALVES + h + 1) * P],
                                           src[:, e, h * P:(h + 1) * P], ident[:])
                return ins

            def adj_tile(u, v, e, l, first, last):
                w = adjT[:, u, e, :, v]
                t = 2 * u + v
                pe.matmul(accA[e][:, 0:D + 1], w, h1[l][:, t, 0:D + 1], start=first, stop=False)
                return pe.matmul(accA[e][:, 0:D], w, h2[l][:, t, :], start=False, stop=last)

            def unit(m, u):
                pe.wait_ge(e2_ok, m * PAIRS + (u + 1))
                for v in range(2):
                    t = 2 * u + v
                    for e in range(2):
                        zhi = Z[:, u, v, e * P:(e + 1) * P].bitcast(BF16).rearrange("p (i w) -> p i w", w=2)[:, :, 1]
                        zlo = E2[:, u, v, e * P:(e + 1) * P]
                        pe.matmul(accE[e][:, 0:D + 1], zhi, h1[0][:, t, 0:D + 1], start=(t == 0), stop=False)
                        pe.matmul(accE[e][:, 0:D], zhi, h2[0][:, t, :], start=False, stop=False)
                        ins = pe.matmul(accE[e][:, 0:D + 1], zlo, h1[0][:, t, 0:D + 1], start=False,
                                        stop=(t == TILES - 1))
                ins.then_inc(unit_done, 1)

            def turn_a(m):
                pe.wait_ge(th_ok, 2 * m + 2)
                pe.wait_ge(tp_ev, 2 * m)
                transposes(tp, Th).then_inc(tp_w, 1)

            pe.wait_ge(consts, 6)
            for i in range(PAIRS + 5):
                if i < PAIRS:
                    pe.wait_ge(hf_ok[0], 2 * i + 2)
                    if i >= 2:
                        pe.wait_ge(hT_ok, i - 1)
                    dst = [tp, dA][i % 2]
                    for h in range(HALVES):
                        for e in range(2):
                            ins = pe.transpose(dst[:, (2 * h + e) * P:(2 * h + e + 1) * P],
                                               hf[:, i % 2, e, h * P:(h + 1) * P], ident[:])
                    ins.then_inc(hT_ps, 1)
                j = i - 1
                if 0 <= j < PAIRS:
                    if j == 0:
                        pe.wait_ge(wprep, 2 * HALVES)
                    pe.wait_ge(hT_ok, j + 1)
                    if j >= 1:
                        pe.wait_ge(sr99_ok, j)
                    for e in range(2):
                        for h in range(HALVES):
                            ins = pe.matmul(dB[0][:, 4 * e:4 * e + 4], hT[:, j % 2, h, e * P:(e + 1) * P],
                                            w4[:, h, :], start=(h == 0), stop=(h == HALVES - 1))
                    ins.then_inc(proj, 1)
                j = i - 2
                if 0 <= j < PAIRS:
                    pe.wait_ge(diag_ok, j + 1)
                    if j >= 1:
                        pe.wait_ge(sl_ok, j)
                    pe.matmul(dB[1][:, 0:2 * P], ones[:], diag[:].rearrange("p e n -> p (e n)"), start=True,
                              stop=True).then_inc(wide, 1)
                j = i - 2
                if 0 <= j < PAIRS:
                    for n, (u0, u1) in enumerate(TURNS):
                        if j == u0:
                            pe.wait_ge(tr_part if u1 < PAIRS else tr_done, n + 1 if u1 < PAIRS else 1)
                    pe.wait_ge(h1_ok[0], j + 1)
                    pe.wait_ge(h2_ok, j + 1)
                    for v in range(2):
                        for e in range(2):
                            last = j == PAIRS - 1 and v == 1
                            ins = adj_tile(j, v, e, 0, j == 0 and v == 0, last)
                            if last:
                                ins.then_inc(a_done, 1)
                j = i - 5
                if 0 <= j < PAIRS:
                    if j == PAIRS - 1:
                        turn_a(0)
                    unit(0, j)

            def adj_part(m, e, u0=0, u1=PAIRS):
                if e == 0:
                    pe.wait_ge(tr_done, m + 1)
                if u0 == 0:
                    pe.wait_ge(th_ok, 2 * m + (e - 1))
                for u in range(u0, u1):
                    for v in range(2):
                        t = 2 * u + v
                        ins = adj_tile(u, v, e, 0, t == 0, t == TILES - 1)
                if u1 == PAIRS:
                    ins.then_inc(a_done, 1)

            def dense_b(m):
                pe.wait_ge(tp_ev, 2 * m + 1)
                pe.wait_ge(ub_ok, 2 * m)
                for e in range(2):
                    for h in range(HALVES):
                        ins = pe.matmul(dB[e][:, 0:HW], TTa[:, e, h, :], wg[:, h, :], start=(h == 0),
                                        stop=(h == HALVES - 1))
                ins.then_inc(db_ok, 1)

            def turn_e(q):
                pe.wait_ge(ae_ok, 2 * q + 2)
                pe.wait_ge(tp_ev, 2 * q + 1)
                transposes(tp, AE).then_inc(tp_w, 1)

            def dense_a(q):
                pe.wait_ge(tp_ev, 2 * q + 2)
                pe.wait_ge(h2_ok, PAIRS + q)
                for e in range(2):
                    for h in range(HALVES):
                        ins = pe.matmul(dA[:, e * D:(e + 1) * D], TTe[:, e, h, :], wsa[:, h, :],
                                        start=(h == 0), stop=(h == HALVES - 1))
                ins.then_inc(da_ok, 1)

            def layer0(m, q):
                adj_part(m, 0)
                adj_part(m, 1, 0, 7)
                turn_e(q)
                adj_part(m, 1, 7)
                dense_a(q)
                for u in range(PAIRS):
                    unit(m, u)
                    if u == 3:
                        turn_a(m)
                    if u == 8:
                        dense_b(m)

            pe.wait_ge(w2_in, 16 * N_W2DMA)
            pe.wait_ge(sr99_ok, PAIRS)
            pe.wait_ge(sl_ok, PAIRS)
            dense_b(0)
            with pe.Fori(0, PAIRS - 1) as q:
                layer0(q + 1, q)

            def units(g, u0, u1):
                pe.wait_ge(h2_ok, PAIRS + u1)
                pe.wait_ge(h1_ok[1], u1)
                for u in range(u0, u1):
                    for v in range(2):
                        for e in range(2):
                            t = 2 * u + v
                            ins = adj_tile(u, v, e, 1, t == 0, t == TILES - 1)
                if u1 == AGROUPS[g][1]:
                    ins.then_inc(grp_done[g], 1)

            def group(m, g):
                pe.wait_ge(adj_ld[g], 16 * m + 16)
                units(g, *AGROUPS[g])

            def turn_p(q):
                pe.wait_ge(pool_ok, 2 * q + 2)
                transposes(tp, AE).then_inc(l1t_w, 1)

            def dense_p(q):
                pe.wait_ge(l1t_ev, q + 1)
                for e in range(2):
                    for h in range(HALVES):
                        ins = pe.matmul(dA[:, e * D:(e + 1) * D], TTa[:, e, h, :], w1[:, h, :],
                                        start=(h == 0), stop=(h == HALVES - 1))
                ins.then_inc(l1d_ok, 1)

            pe.wait_ge(th_ok, TILES)
            pe.wait_ge(adj_ld[0], 16)
            units(0, 0, 2)
            turn_e(PAIRS - 1)
            units(0, 2, 4)
            dense_a(PAIRS - 1)
            group(0, 1)
            pe.wait_ge(adj_ld[2], 16)
            units(2, 8, PAIRS - 1)
            units(2, PAIRS - 1, PAIRS)
            def layer1(q, first=False):
                pe.wait_ge(pt_c, 2 * q + 2)
                group(q + 1, 0)
                turn_p(q)
                group(q + 1, 1)
                group(q + 1, 2)
                if not first:
                    pe.wait_ge(o_ok, q)
                dense_p(q)

            layer1(0, True)
            with pe.Fori(1, PAIRS - 1) as q:
                layer1(q)
            turn_p(PAIRS - 1)
            pe.wait_ge(o_ok, PAIRS - 1)
            dense_p(PAIRS - 1)

        @block.vector
        def _(dve):
            dve.memset(stage[96:P, :, :, QN - 1:QN], 0.0).then_inc(pads, 1)
            dve.memset(xs[96:P, TILES - 1, :], 0.0).then_inc(pads, 1)
            dve.memset(bias4[:, :, 0:1], 0.0)
            dve.memset(bias4[:, :, 3:4], 0.0).then_inc(wchain, 1)

            def pair_stats(i, slot, par, l, src):
                if l:
                    dve.wait_ge(nmr_ok[0], len(BATCHES))
                    dve.wait_ge(x1_ok, i + 1)
                for e in range(2):
                    ins = dve.bn_stats(bst[:, par, e], src[:, e])
                ins.then_inc(bnr[l], 1)
                if l:
                    dve.wait_ge(nmr_ok[0], len(BATCHES))
                dve.wait_ge(bnr[l], i + 1)
                for e in range(2):
                    ins = dve.bn_aggr(mv[:, slot, e], bst[:, par, e])
                ins.then_inc(stats[l], 1)

            def minus_mean(a, b, l, count):
                dve.wait_ge(rstd_ok[l], count)
                dve.scalar_tensor_tensor(out=nmr[:, a:b], in0=mv[:, a:b, :, 0], scalar=-1.0, in1=rstd[:, a:b],
                                         op0=ALU.mult, op1=ALU.mult).then_inc(nmr_ok[l], 1)

            def batch_nmr(n):
                minus_mean(*BATCHES[n], 0, n + 1)

            def pair_nmr(q):
                minus_mean(0, 1, 1, q + 1)

            def second_part(i, par, l, first, dst):
                dve.wait_ge(h1_ok[l], i + 1)
                dve.tensor_tensor(dst, hf[:, par], first, ALU.subtract).then_inc(h2_ok, 1)

            def turn_adj(u0=0, u1=PAIRS, part=None):
                for e in range(2):
                    src = stage[:, e].bitcast(U32).rearrange("p b (u r) -> p b u r", r=QUAD)[:, :, u0:u1]
                    dst = adjT[:, u0:u1, e].rearrange("p u (b c) v -> p b u (c v)", b=4).bitcast(U32)
                    ins = dve.transpose(dst, src)
                if u1 == PAIRS:
                    ins.then_inc(tr_done, 1)
                elif part is not None:
                    ins.then_inc(part, 1)

            def weights():
                dve.wait_ge(w_in, 16 * N_WDMA)
                for h in range(HALVES):
                    for k, dst in enumerate((w4[:, h, 3:4], w4[:, h, 0:1])):
                        dve.tensor_tensor_reduce(out=prod[:, 2 * h + k], in0=wsa[:, h, :], in1=arep[:, k * D:(k + 1) * D],
                                                 scale=1.0, scalar=0.0, op0=ALU.mult, op1=ALU.add,
                                                 accum_out=dst).then_inc(wprep, 1)

            def mask(m, u):
                dve.wait_ge(exp_ok, m * PAIRS + (u + 1))
                for v in range(2):
                    t = 2 * u + v
                    ins = dve.scalar_tensor_tensor(out=Z[:, u, v], in0=adjT[:, u, :, :, v].rearrange("p e i -> p (e i)"),
                                                   scalar=vr[:, t:t + 1], in1=Z[:, u, v], op0=ALU.mult, op1=ALU.mult)
                ins.then_inc(mask_ok, 1)

            def split(m, u):
                dve.wait_ge(mask_ok, m * PAIRS + (u + 1))
                hi = Z[:, u].bitcast(BF16).rearrange("p v (i w) -> p v i w", w=2)[:, :, :, 1]
                dve.tensor_tensor(E2[:, u], Z[:, u], hi, ALU.subtract).then_inc(e2_ok, 1)

            def first_stats(i):
                g = [g for g, (a, b) in enumerate(GROUPS) if a <= i < b][0]
                dve.wait_ge(x_in[g], 16 * (4 if g < len(GROUPS) - 1 else 6))
                if i >= 2:
                    dve.wait_ge(stats[0], i - 1)
                pair_stats(i, i, i % 2, 0, xs[:, 2 * i:2 * i + 2])

            first_stats(0)
            first_stats(1)
            batch_nmr(0)
            batch_nmr(1)
            weights()
            for i in range(PAIRS + 4):
                if i in (1, 3, 6):
                    batch_nmr({1: 2, 3: 3, 6: 4}[i])
                for j in (2 * i + 2, 2 * i + 3):
                    if j < PAIRS:
                        first_stats(j)
                j = i - 2
                if 0 <= j < PAIRS:
                    dve.wait_ge(proj, j + 1)
                    if j == 0:
                        dve.wait_ge(wchain, 1)
                        dve.wait_ge(bias_in, 64)
                    taken = dB[0][:, 0:8].rearrange("p (e k) -> p e k", k=4)
                    dve.tensor_tensor(srw[:, 2 * j:2 * j + 2, :], taken, bias4[:], ALU.add).then_inc(srw_ok, 1)
                    dve.tensor_scalar(sr99[:, 2 * j:2 * j + 2], taken[:, :, 0], 1.0 - SLOPE, None,
                                      ALU.mult).then_inc(sr99_ok, 1)
                    dve.wait_ge(srw_ok, j + 1)
                    if j >= 1:
                        dve.wait_ge(wide, j)
                    for e in range(2):
                        ins = dve.tensor_scalar(diag[:, e], ident[:], srw[:, 2 * j + e, 3:4], None, ALU.mult)
                    ins.then_inc(diag_ok, 1)
                j = i - 1
                if 0 <= j < PAIRS:
                    second_part(j, j % 2, 0, h1[0][:, 2 * j:2 * j + 2, 0:D], h2[0][:, 2 * j:2 * j + 2])
                if i < len(TURNS):
                    if i == 0:
                        dve.wait_ge(adj_in, 16 * 4)
                    turn_adj(*TURNS[i], tr_part)
                j = i - 4
                if 0 <= j < PAIRS:
                    dve.wait_ge(vr_ok, j + 1)
                    if j == 0:
                        dve.wait_ge(tr_done, 1)
                    mask(0, j)
                    split(0, j)
                    if j == 5:
                        dve.wait_ge(adj_in, 16 * 8)
                        dve.wait_ge(stored, 16)
                    if j >= 5:
                        u0, u1 = {5: (0, 2), 6: (2, 4), 7: (4, 6)}.get(j, (j - 2, j - 1))
                        dve.wait_ge(unit_done, u1)
                        turn_adj(u0, u1)
            for u in (PAIRS - 2, PAIRS - 1):
                dve.wait_ge(unit_done, u + 1)
                turn_adj(u, u + 1)

            def degrees(m):
                dve.wait_ge(th_ok, 2 * m + 2)
                dve.tensor_scalar(degm[:], Th[:, :, ones_col], 1.0, None, ALU.max).then_inc(deg_c, 1)
                dve.wait_ge(deg_c, m + 1)
                dve.reciprocal(dr[:, bass.ds(2 * m, 2)], degm[:]).then_inc(deg_ok, 1)

            def row_sums(q):
                dve.wait_ge(unit_done, q * PAIRS + PAIRS)
                for e in range(2):
                    ins = dve.scalar_tensor_tensor(out=ssum[:, e:e + 1], in0=el[:, bass.ds(2 * q + e, 1)],
                                                   scalar=SUM_EPS, in1=accE[e][:, ones_col:ones_col + 1],
                                                   op0=ALU.mult, op1=ALU.add)
                ins.then_inc(rs_c, 1)
                dve.wait_ge(rs_c, q + 1)
                dve.reciprocal(rs[:], ssum[:]).then_inc(rs_ok, 1)

            def gate_args(q):
                dve.wait_ge(db_ok, q + 1)
                for e in range(2):
                    ins = dve.tensor_tensor(zg[:, e:e + 1], dB[e][:, D:HW].rearrange("p (a k) -> p a k", a=1),
                                            srw[:, bass.ds(2 * q + e, 1), 1:3], ALU.add)
                ins.then_inc(zg_ok, 1)

            def gates(q):
                dve.wait_ge(eg_ok, q + 1)
                dve.tensor_scalar(eg1[:], eg[:], 1.0, None, ALU.add).then_inc(gate_c, 1)
                dve.wait_ge(gate_c, q + 1)
                dve.reciprocal(gate[:], eg1[:]).then_inc(gate_ok, 1)

            def mix(q):
                dve.wait_ge(ub_ok, 2 * q + 2)
                dve.wait_ge(w2_in, 16 * N_W2DMA)
                for e in range(2):
                    dve.scalar_tensor_tensor(out=wm[:, e], in0=bgrep[:], scalar=gate[:, e, 1:2], in1=ub[:, e],
                                             op0=ALU.mult, op1=ALU.add).then_inc(wm_c, 1)
                dve.wait_ge(da_ok, q + 1)
                for e in range(2):
                    dve.wait_ge(wm_c, 2 * q + (e + 1))
                    dve.scalar_tensor_tensor(out=wm[:, e], in0=dA[:, e * D:(e + 1) * D],
                                             scalar=gate[:, e, 0:1], in1=wm[:, e], op0=ALU.mult,
                                             op1=ALU.add).then_inc(wm_ok, 1)

            def residual(q):
                dve.wait_ge(h2_ok, PAIRS + q)
                dve.wait_ge(wx_ok, q + 1)
                dve.tensor_scalar(wm[:], wx[:], 0.5, 0.5, ALU.mult, ALU.add).then_inc(x1_c, 1)
                dve.wait_ge(x1_c, q + 1)
                dve.tensor_tensor(xs[:, bass.ds(2 * q, 2)], xs[:, bass.ds(2 * q, 2)], wm[:],
                                  ALU.add).then_inc(x1_ok, 1)
                pair_stats(q, 0, 0, 1, xs[:, bass.ds(2 * q, 2)])

            def later_second(q):
                second_part(q, 0, 1, h1[1][:, bass.ds(2 * q, 2), 0:D], h2[1][:, bass.ds(2 * q, 2)])

            def next_adj(m, adj_count):
                dve.wait_ge(adj_in, adj_count)
                dve.wait_ge(a_done, 2 * m)
                dve.wait_ge(stored, 16 * m)
                dve.wait_ge(mask_ok, m * PAIRS)
                turn_adj()

            def layer0(m, q, p, adj_count, sums_at=8):
                dve.wait_ge(tr_done, m + 1)
                for u in range(PAIRS + 1):
                    if u < PAIRS:
                        mask(m, u)
                    if u >= 1:
                        split(m, u - 1)
                    if p is not None:
                        if u == 1:
                            pair_nmr(p)
                        if u == 9:
                            later_second(p)
                    if u == sums_at:
                        row_sums(q)
                        gate_args(q)
                    if u == sums_at + 2:
                        gates(q)
                mix(q)
                degrees(m)
                if adj_count is not None:
                    next_adj(m + 1, adj_count)
                residual(q)

            degrees(0)
            dve.wait_ge(vr_ok, PAIRS + 1)
            layer0(1, 0, None, 64 * 3, 0)
            with dve.Fori(0, PAIRS - 4) as q:
                layer0(q + 2, q + 1, q, q * 64 + 256)
            last = PAIRS - 1
            layer0(last - 1, last - 2, last - 3, 64 * PAIRS + 128)
            layer0(last, last - 1, last - 2, None)
            pair_nmr(last - 1)
            row_sums(last)
            gate_args(last)
            later_second(last - 1)
            gates(last)
            mix(last)
            residual(last)
            pair_nmr(last)
            later_second(last)

            def pooled(m):
                dve.wait_ge(grp_done[-1], m + 1)
                dve.wait_ge(hp_ok, m + 1)
                dve.tensor_copy(drp[:], dr[:, bass.ds(2 * m, 2)]).then_inc(drp_ok, 1)
                for e in range(2):
                    dve.tensor_tensor(wm[:, e], accA[e][:, 0:D], hp[:, e], ALU.add).then_inc(pt_c, 1)
                dve.wait_ge(drp_ok, m + 1)
                for e in range(2):
                    dve.wait_ge(pt_c, 2 * m + (e + 1))
                    dve.scalar_tensor_tensor(out=AE[:, e], in0=wm[:, e], scalar=drp[:, e:e + 1], in1=hp[:, e],
                                             op0=ALU.mult, op1=ALU.add).then_inc(pool_ok, 1)

            def output(q, first=False):
                dve.wait_ge(l1d_ok, q + 1)
                dve.tensor_tensor(wx[:], dA[:].rearrange("p (e d) -> p e d", e=2),
                                  bass.AP(b1rep[:].tensor, 0, [[D, P], [0, 2], [1, D]]), ALU.add).then_inc(ob_c, 1)
                dve.wait_ge(ob_c, q + 1)
                if not first:
                    dve.wait_ge(o_out, 64 * q)
                dve.scalar_tensor_tensor(out=osb[:], in0=wx[:], scalar=0.0, in1=xs[:, bass.ds(2 * q, 2)],
                                         op0=ALU.max, op1=ALU.add).then_inc(o_ok, 1)

            pooled(0)
            dve.wait_ge(l1t_w, 1)
            pooled(1)
            output(0, True)
            with dve.Fori(1, PAIRS - 1) as q:
                dve.wait_ge(l1t_w, q + 1)
                pooled(q + 1)
                output(q)
            output(PAIRS - 1)


_INS = ['x', 'adj', 'L0_gnn_W_sa', 'L0_gnn_a_sa', 'L0_gnn_W_gcnb', 'L0_gnn_b_gcnb', 'L0_gnn_Wa', 'L0_gnn_ba',
        'L0_gnn_Wb', 'L0_gnn_bb', 'L1_gnn_W', 'L1_gnn_b']


def kernel(**inputs):
    import numpy as _np
    import concourse.bacc as _bacc
    from concourse import mybir as _mybir
    from concourse.bass_utils import run_bass_kernel_spmd as _run

    nc = _bacc.Bacc("TRN2", target_bir_lowering=False, num_devices=1)
    arrays, args = {}, []
    for name in _INS:
        a = _np.ascontiguousarray(inputs[name])
        arrays[f"in_{name}_dram"] = a
        args.append(nc.dram_tensor(f"in_{name}_dram", a.shape, _mybir.dt.from_np(a.dtype), kind="ExternalInput").ap())
    shape = inputs['x'].shape
    args.append(nc.dram_tensor("out_0_dram", shape, _mybir.dt.float32, kind="ExternalOutput").ap())
    gnn_kernel(nc, *args)
    r = _run(nc, [arrays], core_ids=[0])
    return r.results[0]["out_0_dram"]
```

```python
from contextlib import ExitStack

import concourse.bass as bass
from concourse import mybir

F32 = mybir.dt.float32
F16 = mybir.dt.float16
BF16 = mybir.dt.bfloat16
U32 = mybir.dt.uint32
ALU = mybir.AluOpType
ACT = mybir.ActivationFunctionType

P = 128
QUAD = 32
LN_EPS = 1e-5
SUM_EPS = 1e-5
SLOPE = 0.01


def gnn_kernel(nc, x, adj, W_sa, a_sa, W_g, b_g, Wa, ba, Wb, bb, W1, b1, out):
    N, D = x.shape
    PAIRS = -(-N // (2 * P))
    TILES = 2 * PAIRS
    QN = TILES * QUAD
    assert 16 * N < 65504
    HALVES = D // P
    HW = D + 2
    ones_col = D
    GROUPS = [(0, 2), (2, 4), (4, 8), (8, PAIRS)]
    TURNS = [(0, 4), (4, 9), (9, PAIRS)]
    BATCHES = [(0, 1), (1, 2), (2, 4), (4, 8), (8, PAIRS)]
    AGROUPS = [(0, 4), (4, 8), (8, PAIRS)]

    with ExitStack() as ctx:
        def sb(name, shape, dt=F32):
            return ctx.enter_context(nc.sbuf_tensor(name, shape, dt))

        def ps(name):
            return ctx.enter_context(nc.psum_tensor(name, [P, 512], F32))

        def sem(name):
            return ctx.enter_context(nc.semaphore(name))

        adjT_store = nc.dram_tensor("adjT_store", [PAIRS, P, PAIRS * 256], U32, kind="Internal").ap()

        xs = sb("xs", [P, TILES, D])
        h1 = [sb(f"h1_{l}", [P, TILES, HW], F16) for l in range(2)]
        h2 = [sb(f"h2_{l}", [P, TILES, D], F16) for l in range(2)]
        stage = sb("stage", [P, 2, 4, QN], BF16)
        adjT = sb("adjT", [P, PAIRS, 2, P, 2], BF16)
        Z = sb("Z", [P, PAIRS, 2, 2 * P])
        E2 = sb("E2", [P, PAIRS, 2, 2 * P], BF16)
        sl = sb("sl", [P, TILES * P])
        slp = sb("slp", [P, 2 * P])
        srw = sb("srw", [P, TILES, 4])
        sr99 = sb("sr99", [P, TILES])
        vr = sb("vr", [P, TILES])
        el = sb("el", [P, TILES])
        bst = sb("bst", [P, 2, 2, 6])
        mv = sb("mv", [P, PAIRS, 2, 2])
        ve = sb("ve", [P, PAIRS, 2])
        rstd = sb("rstd", [P, PAIRS, 2])
        nmr = sb("nmr", [P, PAIRS, 2])
        unused = sb("unused", [P, 1])
        halfs = sb("halfs", [P, PAIRS, 2])
        epss = sb("epss", [P, PAIRS, 2])
        hf = sb("hf", [P, 2, 2, D])
        hT = sb("hT", [P, 2, HALVES, 2 * P])
        ident = sb("ident", [P, P])
        wsa = sb("wsa", [P, HALVES, D])
        wg = sb("wg", [P, HALVES, HW])
        w1 = sb("w1", [P, HALVES, D])
        w4 = sb("w4", [P, HALVES, 4])
        diag = sb("diag", [P, 2, P])
        ones = sb("ones", [P, P])
        arep = sb("arep", [P, 2 * D])
        prod = sb("prod", [P, 2 * HALVES, D])
        bias4 = sb("bias4", [P, 2, 4])
        bgrep = sb("bgrep", [P, D])
        b1rep = sb("b1rep", [P, D])
        AE = sb("AE", [P, 2, D])
        Ta = sb("Ta", [P, 2, HALVES, 2 * P], F16)
        Te = sb("Te", [P, 2, 2, HALVES, P], F16)
        wabs = sb("wabs", [P, 3])
        wdiag = sb("wdiag", [P, 3, P])
        wmax = sb("wmax", [P, 3])
        wmax0 = sb("wmax0", [P, 3])
        winv = sb("winv", [P, 3])
        w16 = [sb(f"w16_{k}", [P, 2, HALVES, n], F16) for k, n in enumerate((D, HW, D))]
        degm = sb("degm", [P, 2])
        drp = sb("drp", [P, 2])
        ssum = sb("ssum", [P, 2])
        rs = sb("rs", [P, 2])
        zg = sb("zg", [P, 2, 2])
        eg = sb("eg", [P, 2, 2])
        eg1 = sb("eg1", [P, 2, 2])
        gate = sb("gate", [P, 2, 2])
        gscale = sb("gscale", [P, 2, 2])
        ub = sb("ub", [P, 2, D])
        wm = sb("wm", [P, 2, D])
        wx = sb("wx", [P, 2, D])
        hp = sb("hp", [P, 2, D])
        osb = sb("osb", [P, 2, D])

        accE = [ps("accE0"), ps("accE1")]
        accA = [ps("accA0"), ps("accA1")]
        tp = ps("tp")
        dB = [ps("dB0"), ps("dB1")]
        dA = ps("dA")

        x_in = [sem(f"x_in{g}") for g in range(len(GROUPS))]
        w_in = sem("w_in")
        bias_in = sem("bias_in")
        w2_in = sem("w2_in")
        pads = sem("pads")
        consts = sem("consts")
        id0 = sem("id0")
        wprep = sem("wprep")
        bias_pad = sem("bias_pad")
        stats = [sem(f"stats_{l}") for l in range(2)]
        bnr = [sem(f"bnr_{l}") for l in range(2)]
        vplus = [sem(f"vplus_{l}") for l in range(2)]
        rstd_ok = [sem(f"rstd_ok_{l}") for l in range(2)]
        nmr_ok = [sem(f"nmr_ok_{l}") for l in range(2)]
        hf_ok = [sem(f"hf_ok_{l}") for l in range(2)]
        h1_ok = [sem(f"h1_ok_{l}") for l in range(2)]
        h2_ok = sem("h2_ok")
        hT_ps = sem("hT_ps")
        hT_ok = sem("hT_ok")
        proj = sem("proj")
        diag_ok = sem("diag_ok")
        wide = sem("wide")
        srw_ok = sem("srw_ok")
        sl_ok = sem("sl_ok")
        adj_in = sem("adj_in")
        tr_done = sem("tr_done")
        tr_part = sem("tr_part")
        stored = sem("stored")
        a_done = sem("a_done")
        slp_ok = sem("slp_ok")
        vr_ok = sem("vr_ok")
        sr99_ok = sem("sr99_ok")
        pl_ok = sem("pl_ok")
        exp_ok = sem("exp_ok")
        mask_ok = sem("mask_ok")
        e2_ok = sem("e2_ok")
        unit_done = sem("unit_done")
        th_ok = sem("th_ok")
        deg_c = sem("deg_c")
        tp_w = sem("tp_w")
        tp_ev = sem("tp_ev")
        db_ok = sem("db_ok")
        da_ok = sem("da_ok")
        rs_c = sem("rs_c")
        rs_ok = sem("rs_ok")
        ae_ok = sem("ae_ok")
        zg_ok = sem("zg_ok")
        eg_ok = sem("eg_ok")
        gate_c = sem("gate_c")
        gate_ok = sem("gate_ok")
        gscale_ok = sem("gscale_ok")
        wabs_ok = sem("wabs_ok")
        wdiag_ok = sem("wdiag_ok")
        wspread = sem("wspread")
        wmax_c = sem("wmax_c")
        winv_ok = sem("winv_ok")
        w16a = sem("w16a")
        w16b = sem("w16b")
        ta2_ok = sem("ta2_ok")
        te2_ok = sem("te2_ok")
        l1t_2 = sem("l1t_2")
        end_2 = sem("end_2")
        ub_ok = sem("ub_ok")
        wm_c = sem("wm_c")
        wm_ok = sem("wm_ok")
        wx_ok = sem("wx_ok")
        x1_c = sem("x1_c")
        x1_ok = sem("x1_ok")
        adj_ld = [sem(f"adj_ld{g}") for g in range(len(AGROUPS))]
        grp_done = [sem(f"grp_done{g}") for g in range(len(AGROUPS))]
        hp_ok = sem("hp_ok")
        pt_c = sem("pt_c")
        pool_ok = sem("pool_ok")
        drp_ok = sem("drp_ok")
        half_done = sem("half_done")
        end_t = sem("end_t")
        end_ev = sem("end_ev")
        end_d = sem("end_d")
        end_o = sem("end_o")
        l1t_w = sem("l1t_w")
        l1t_ev = sem("l1t_ev")
        l1d_ok = sem("l1d_ok")
        ob_c = sem("ob_c")
        o_ok = sem("o_ok")
        o_out = sem("o_out")

        N_WDMA = 4
        N_W2DMA = 6

        def load_x(engine, g, quadrants=range(4)):
            u0, u1 = GROUPS[g]
            for b in quadrants:
                full = u1 if (b < 3 or u1 < PAIRS) else PAIRS - 1
                src = bass.AP(x.tensor, (QN * b + 64 * u0) * D, [[2 * D, QUAD], [64 * D, full - u0], [1, 2 * D]])
                dst = xs[32 * b:32 * b + 32, 2 * u0:2 * full, :].rearrange("p (u v) d -> p u (v d)", v=2)
                engine.dma_start(dst, src).then_inc(x_in[g], 16)
                if full < u1:
                    r0 = QN * b + 64 * full
                    src = bass.AP(x.tensor, r0 * D, [[2 * D, QUAD - 1], [1, 2 * D]])
                    dst = xs[96:96 + QUAD - 1, 2 * full:2 * u1, :].rearrange("p v d -> p (v d)")
                    engine.dma_start(dst, src).then_inc(x_in[g], 16)
                    src = bass.AP(x.tensor, (N - 1) * D, [[D, 1], [1, D]])
                    engine.dma_start(xs[P - 1:P, 2 * full, :], src).then_inc(x_in[g], 16)

        def batch_of(i):
            return [n for n, (a, b) in enumerate(BATCHES) if a <= i < b][0]

        block = ctx.enter_context(nc.Block())

        @block.sync
        def _(sp):
            load_x(sp, 0, (0, 1))
            sp.wait_ge(pads, 2)
            for g in range(1, len(GROUPS)):
                load_x(sp, g)
                if g == 1:
                    for e in range(2):
                        for k, w in enumerate((ba, bb)):
                            src = bass.AP(w.tensor, 0, [[0, P], [1, 1]])
                            sp.dma_start(bias4[:, e, 1 + k:2 + k], src).then_inc(bias_in, 16)
                    sp.wait_ge(w_in, 16 * N_WDMA)
            for k, w in enumerate((Wa, Wb)):
                sp.dma_start(wg[:, :, D + k], w[0, 0:D].rearrange("(h p) -> p h", p=P),
                             allow_slow_non_contiguous=True).then_inc(w2_in, 16)
            sp.dma_start(wg[:, :, 0:D], W_g.rearrange("(h p) o -> p h o", p=P)).then_inc(w2_in, 16)
            sp.dma_start(bgrep[:], bass.AP(b_g.tensor, 0, [[0, P], [1, D]])).then_inc(w2_in, 16)
            sp.dma_start(w1[:], W1.rearrange("(h p) o -> p h o", p=P)).then_inc(w2_in, 16)
            sp.dma_start(b1rep[:], bass.AP(b1.tensor, 0, [[0, P], [1, D]])).then_inc(w2_in, 16)
            with sp.Fori(0, PAIRS) as q:
                sp.wait_ge(tr_done, q + 1)
                sp.dma_start(adjT_store[bass.ds(q, 1)].rearrange("a p n -> p (a n)"),
                             adjT[:].rearrange("p u e i v -> p (u e i v)").bitcast(U32)).then_inc(stored, 16)
            sp.wait_ge(stored, 16 * PAIRS)

            def load_pair(q):
                for g, (u0, u1) in enumerate(AGROUPS):
                    yield g, (adjT[:, u0:u1].rearrange("p u e i v -> p (u e i v)").bitcast(U32),
                              adjT_store[bass.ds(q, 1), :, 256 * u0:256 * u1].rearrange("a p n -> p (a n)"))

            sp.wait_ge(mask_ok, PAIRS * PAIRS)
            sp.wait_ge(a_done, TILES)
            for g, (dst, src) in load_pair(0):
                sp.dma_start(dst, src).then_inc(adj_ld[g], 16)

            with sp.Fori(0, PAIRS - 1) as q:
                for g, (dst, src) in load_pair(q + 1):
                    sp.wait_ge(grp_done[g], q + 1)
                    sp.dma_start(dst, src).then_inc(adj_ld[g], 16)

        @block.gpsimd
        def _(pool):
            pool.memset(ident[:], 0.0).then_inc(id0, 1)
            pool.memset(ones[:], 1.0).then_inc(consts, 1)
            pool.memset(halfs[:], -0.5).then_inc(consts, 1)
            pool.memset(epss[:], LN_EPS).then_inc(consts, 1)
            for l in range(2):
                pool.memset(h1[l][:, :, ones_col:HW], 1.0).then_inc(consts, 1)
            pool.wait_ge(id0, 1)
            pool.affine_select(out=ident[:], in_=ident[:], compare_op=ALU.not_equal, fill=1.0, base=0,
                               pattern=[[-1, P]], channel_multiplier=1).then_inc(consts, 1)

            def load_adj(q, quadrants=range(4)):
                for b in quadrants:
                    w = QN if b < 3 else QN - 1
                    src = bass.AP(adj.tensor, q * (64 * N) + QN * b, [[2 * N, QUAD], [N, 2], [QN * N, 4], [1, w]])
                    pool.dma_start(stage[32 * b:32 * b + 32, :, :, 0:w], src).then_inc(adj_in, 16)

            def load_last_adj():
                for b in range(4):
                    w = QN if b < 3 else QN - 1
                    base = (PAIRS - 1) * 64 * N + QN * b
                    for e, r0, r1, rows in ((0, 0, 4, QUAD), (1, 0, 3, QUAD), (1, 3, 4, QUAD - 1)):
                        src = bass.AP(adj.tensor, base + (e + r0 * QN) * N,
                                      [[2 * N, rows], [QN * N, r1 - r0], [1, w]])
                        pool.dma_start(stage[32 * b:32 * b + rows, e, r0:r1, 0:w], src).then_inc(adj_in, 16)

            def inv_std(q):
                pool.wait_ge(stats[1], q + 1)
                pool.tensor_tensor(ve[:, 0], mv[:, 0, :, 1], epss[:, 0], ALU.add).then_inc(vplus[1], 1)
                pool.wait_ge(vplus[1], q + 1)
                pool.wait_ge(h2_ok, PAIRS + q)
                pool.tensor_tensor(rstd[:, 0], ve[:, 0], halfs[:, 0], ALU.pow).then_inc(rstd_ok[1], 1)

            def inv_stds(n):
                a, b = BATCHES[n]
                pool.wait_ge(stats[0], b)
                pool.tensor_tensor(ve[:, a:b], mv[:, a:b, :, 1], epss[:, 0:b - a], ALU.add).then_inc(vplus[0], 1)
                pool.wait_ge(vplus[0], n + 1)
                pool.tensor_tensor(rstd[:, a:b], ve[:, a:b], halfs[:, 0:b - a], ALU.pow).then_inc(rstd_ok[0], 1)

            def first_part(i, par, l, dst):
                pool.wait_ge(hf_ok[l], 2 * i + 2)
                pool.tensor_copy(dst, hf[:, par]).then_inc(h1_ok[l], 1)

            def later_first(q):
                first_part(q, 0, 1, h1[1][:, bass.ds(2 * q, 2), 0:D])

            pool.wait_ge(consts, 6)
            inv_stds(0)
            inv_stds(1)
            pool.wait_ge(pads, 1)
            load_adj(0)
            for i in range(PAIRS):
                first_part(i, i % 2, 0, h1[0][:, 2 * i:2 * i + 2, 0:D])
                if i in (0, 2, 5):
                    inv_stds({0: 2, 2: 3, 5: 4}[i])
                if 4 <= i < 8:
                    pool.wait_ge(tr_done, 1)
                    load_adj(1, quadrants=(i - 4,))

            pool.wait_ge(tr_done, 2)
            load_adj(2)
            with pool.Fori(0, PAIRS - 4) as q:
                inv_std(q)
                pool.wait_ge(tr_done, q + 3)
                load_adj(q + 3)
                later_first(q)
            inv_std(PAIRS - 4)
            pool.wait_ge(tr_done, PAIRS - 1)
            pool.memset(stage[:, 1, 3, :], 0.0).then_inc(pads, 1)
            pool.wait_ge(pads, 3)
            load_last_adj()
            later_first(PAIRS - 4)
            for q in range(PAIRS - 3, PAIRS):
                inv_std(q)
                if q < PAIRS - 1:
                    later_first(q)

            def self_h(q):
                pool.tensor_tensor(hp[:], h1[1][:, bass.ds(2 * q, 2), 0:D], h2[1][:, bass.ds(2 * q, 2), :],
                                   ALU.add).then_inc(hp_ok, 1)
            pool.wait_ge(h2_ok, 2 * PAIRS)
            self_h(0)
            with pool.Fori(0, PAIRS - 1) as q:
                pool.wait_ge(pool_ok, 2 * q + 2)
                self_h(q + 1)

        @block.scalar
        def _(act):
            def wdma(dst, src, scattered=False):
                act.dma_start(dst, src, allow_slow_non_contiguous=scattered).then_inc(w_in, 16)

            load_x(act, 0, (2, 3))
            rep = lambda t, off, n: bass.AP(t.tensor, off, [[0, P], [1, n]])
            for k, w in enumerate((Wa, Wb)):
                wdma(w4[:, :, 1 + k], w[0, D:2 * D].rearrange("(h p) -> p h", p=P), True)
            wdma(wsa[:], W_sa.rearrange("(h p) o -> p h o", p=P))
            wdma(arep[:], rep(a_sa, 0, 2 * D))
            act.wait_ge(consts, 6)
            act.activation(unused[:], halfs[:, 0, 0:1], ACT.Exp)

            def norm(i, slot, par, l, src):
                if l:
                    act.wait_ge(hT_ps, PAIRS)
                act.wait_ge(nmr_ok[l], i + 1 if l else batch_of(i) + 1)
                for e in range(2):
                    act.activation(hf[:, par, e], src[:, e], ACT.Relu, bias=nmr[:, slot, e:e + 1],
                                   scale=rstd[:, slot, e:e + 1]).then_inc(hf_ok[l], 1)

            def leaky(m, u, fresh):
                if not fresh:
                    act.wait_ge(unit_done, (m - 1) * PAIRS + (u + 1))
                for v in range(2):
                    t = 2 * u + v
                    ins = act.activation(Z[:, u, v], slp[:], ACT.Relu, bias=sr99[:, t:t + 1], scale=1.0 - SLOPE)
                ins.then_inc(pl_ok, 1)

            def expo(m, u):
                act.wait_ge(pl_ok, m * PAIRS + (u + 1))
                act.activation(Z[:, u], Z[:, u], ACT.Exp, scale=-1.0).then_inc(exp_ok, 1)

            for i in range(PAIRS + 4):
                if 6 <= i < 9:
                    act.wait_ge(winv_ok, 1)
                    k = i - 6
                    act.activation(w16[k][:, 0], (wsa, wg, w1)[k][:], ACT.Copy,
                                   scale=winv[:, k:k + 1]).then_inc(w16a, 1)
                if i < PAIRS:
                    act.wait_ge(x_in[[g for g, (a, b) in enumerate(GROUPS) if a <= i < b][0]],
                                16 * (4 if i < GROUPS[-1][0] else 6))
                    if i >= 2:
                        act.wait_ge(h2_ok, i - 1)
                        act.wait_ge(hT_ps, i - 1)
                    norm(i, i, i % 2, 0, xs[:, 2 * i:2 * i + 2])
                j = i - 1
                if 0 <= j < PAIRS:
                    act.wait_ge(hT_ps, j + 1)
                    if j >= 2:
                        act.wait_ge(proj, j - 1)
                    act.activation(hT[:, j % 2], [tp, dA][j % 2][:].rearrange("p (h n) -> p h n", h=HALVES),
                                   ACT.Copy).then_inc(hT_ok, 1)
                j = i - 3
                if 0 <= j < PAIRS:
                    act.wait_ge(srw_ok, j + 1)
                    act.activation(vr[:, 2 * j:2 * j + 2], srw[:, 2 * j:2 * j + 2, 0], ACT.Exp,
                                   scale=-SLOPE).then_inc(vr_ok, 1)
                    act.wait_ge(wide, j + 1)
                    act.activation(sl[:, 2 * P * j:2 * P * (j + 1)], dB[1][:, 0:2 * P],
                                   ACT.Copy).then_inc(sl_ok, 1)
                    if j == 0:
                        act.wait_ge(sl_ok, 1)
                        act.activation(slp[:], sl[:, 0:2 * P], ACT.Copy).then_inc(slp_ok, 1)
                        act.wait_ge(slp_ok, 1)
                    act.wait_ge(sr99_ok, j + 1)
                    leaky(0, j, True)
                j = i - 4
                if 0 <= j < PAIRS:
                    expo(0, j)
            act.wait_ge(sl_ok, PAIRS)


            def sums_out(m, h, first=False):
                act.wait_ge(a_done, 2 * m + (h + 1))
                if h == 0 and not first:
                    act.wait_ge(db_ok, m)
                act.activation(Ta[:, 0, h], accA[h][:, 0:2 * P], ACT.Copy).then_inc(th_ok, 1)

            def attn_out(q):
                act.wait_ge(rs_ok, q + 1)
                for e in range(2):
                    act.activation(AE[:, e], accE[e][:, 0:D], ACT.Copy, scale=rs[:, e:e + 1]).then_inc(ae_ok, 1)

            def turned_e(q):
                act.wait_ge(tp_w, q + 1)
                act.activation(Te[:, 0].rearrange("p e h i -> p (e h i)"), tp[:], ACT.Copy).then_inc(tp_ev, 1)

            def gate_exp(q):
                act.wait_ge(zg_ok, q + 1)
                act.activation(eg[:], zg[:], ACT.Exp, scale=-1.0).then_inc(eg_ok, 1)

            def gated_b(q):
                act.wait_ge(gscale_ok, q + 1)
                act.wait_ge(db_ok, q + 1)
                for e in range(2):
                    act.activation(ub[:, e], dB[e][:, 0:D], ACT.Copy, scale=gscale[:, e, 1:2]).then_inc(ub_ok, 1)

            def half_tanh(q):
                act.wait_ge(wm_ok, 2 * q + 2)
                act.activation(wx[:], wm[:], ACT.Tanh, scale=0.5).then_inc(wx_ok, 1)

            def norm_later(q):
                act.wait_ge(x1_ok, q + 1)
                act.wait_ge(h2_ok, PAIRS + q)
                norm(q, 0, 0, 1, xs[:, bass.ds(2 * q, 2)])

            def layer0(m, q, p, sums_at=10, turn_at=PAIRS):
                act.activation(slp[:], sl[:, bass.ds(m * (2 * P), 2 * P)], ACT.Copy).then_inc(slp_ok, 1)
                act.wait_ge(slp_ok, m + 1)
                for u in range(PAIRS + 1):
                    if u < PAIRS:
                        leaky(m, u, False)
                    if u >= 1:
                        expo(m, u - 1)
                    if p is not None and u == 3:
                        norm_later(p)
                    if u == sums_at:
                        attn_out(q)
                        gate_exp(q)
                    if u == turn_at:
                        gated_b(q)
                        sums_out(m, 0)
                        turned_e(q)
                sums_out(m, 1)
                half_tanh(q)

            sums_out(0, 0, True)
            sums_out(0, 1)
            act.activation(el[:], srw[:, :, 3], ACT.Exp, scale=SLOPE).then_inc(vr_ok, 1)
            layer0(1, 0, None, 3, 8)
            with act.Fori(0, PAIRS - 2) as q:
                layer0(q + 2, q + 1, q)
            last = PAIRS - 1
            norm_later(last - 1)
            attn_out(last)
            gate_exp(last)
            gated_b(last)
            turned_e(last)
            half_tanh(last)
            norm_later(last)

            def turned_p(q):
                act.wait_ge(l1t_w, q + 1)
                act.activation(Te[:, 0].rearrange("p e h i -> p (e h i)"), tp[:], ACT.Copy).then_inc(l1t_ev, 1)

            def store_out(q):
                act.wait_ge(o_ok, q + 1)
                dst = bass.AP(out.tensor, q * (64 * D), [[QN * D, 4], [2 * D, QUAD], [1, 2 * D]])
                act.dma_start(dst, osb[:].rearrange("p e d -> p (e d)")).then_inc(o_out, 16)

            last = PAIRS - 1
            turned_p(0)
            with act.Fori(0, last - 1) as q:
                store_out(q)
                turned_p(q + 1)
            store_out(last - 1)
            for e in range(2):
                act.wait_ge(end_t, e + 1)
                act.activation(Ta[:, 0, e], dB[e][:, 0:2 * P], ACT.Copy).then_inc(end_ev, 1)
            act.wait_ge(end_o, 1)
            dst = bass.AP(out.tensor, last * (64 * D), [[QN * D, 4], [2 * D, QUAD], [1, D]])
            act.dma_start(dst, ub[:, 0]).then_inc(o_out, 16)
            act.wait_ge(end_o, 2)
            dst = bass.AP(out.tensor, last * (64 * D) + D, [[QN * D, 3], [2 * D, QUAD], [1, D]])
            act.dma_start(dst, ub[0:3 * QUAD, 1]).then_inc(o_out, 16)
            dst = bass.AP(out.tensor, last * (64 * D) + (3 * QN + 1) * D, [[2 * D, QUAD - 1], [1, D]])
            act.dma_start(dst, ub[3 * QUAD:P - 1, 1]).then_inc(o_out, 16)
            act.wait_ge(o_out, 16 * (last + 3))

        @block.tensor
        def _(pe):
            def transposes(dst, src):
                for e in range(2):
                    for h in range(HALVES):
                        ins = pe.transpose(dst[:, (e * HALVES + h) * P:(e * HALVES + h + 1) * P],
                                           src[:, e, h * P:(h + 1) * P], ident[:])
                return ins

            def adj_turned(u, v, h):
                rows = adjT[:, u, :, :, v].rearrange("p e i -> p (e i)")
                t = 2 * u + v
                cols = slice(h * P, (h + 1) * P)
                pe.matmul(accA[h][:, 0:2 * P], h1[0][:, t, cols], rows, start=(t == 0), stop=False)
                return pe.matmul(accA[h][:, 0:2 * P], h2[0][:, t, cols], rows, start=False, stop=(t == TILES - 1))

            def adj_tile(u, v, e):
                w = adjT[:, u, e, :, v]
                t = 2 * u + v
                pe.matmul(accA[e][:, 0:D + 1], w, h1[1][:, t, 0:D + 1], start=(t == 0), stop=False)
                return pe.matmul(accA[e][:, 0:D], w, h2[1][:, t, :], start=False, stop=(t == TILES - 1))

            def unit(m, u):
                pe.wait_ge(e2_ok, m * PAIRS + (u + 1))
                for v in range(2):
                    t = 2 * u + v
                    for e in range(2):
                        zhi = Z[:, u, v, e * P:(e + 1) * P].bitcast(BF16).rearrange("p (i w) -> p i w", w=2)[:, :, 1]
                        zlo = E2[:, u, v, e * P:(e + 1) * P]
                        pe.matmul(accE[e][:, 0:D + 1], zhi, h1[0][:, t, 0:D + 1], start=(t == 0), stop=False)
                        pe.matmul(accE[e][:, 0:D], zhi, h2[0][:, t, :], start=False, stop=False)
                        ins = pe.matmul(accE[e][:, 0:D + 1], zlo, h1[0][:, t, 0:D + 1], start=False,
                                        stop=(t == TILES - 1))
                ins.then_inc(unit_done, 1)

            def dense(dst, x1, x2, w):
                for h in range(HALVES):
                    pe.matmul(dst, x1(h), w[:, 0, h, :], start=(h == 0), stop=False)
                    pe.matmul(dst, x1(h), w[:, 1, h, :], start=False, stop=False)
                    ins = pe.matmul(dst, x2(h), w[:, 0, h, :], start=False, stop=(h == HALVES - 1))
                return ins

            pe.wait_ge(consts, 6)
            for i in range(PAIRS + 5):
                if i == 4:
                    pe.wait_ge(wdiag_ok, 1)
                    pe.matmul(accE[0][:, 0:3 * P], ones[:], wdiag[:].rearrange("p k n -> p (k n)"), start=True,
                              stop=True).then_inc(wspread, 1)
                if i < PAIRS:
                    pe.wait_ge(hf_ok[0], 2 * i + 2)
                    if i >= 2:
                        pe.wait_ge(hT_ok, i - 1)
                    dst = [tp, dA][i % 2]
                    for h in range(HALVES):
                        for e in range(2):
                            ins = pe.transpose(dst[:, (2 * h + e) * P:(2 * h + e + 1) * P],
                                               hf[:, i % 2, e, h * P:(h + 1) * P], ident[:])
                    ins.then_inc(hT_ps, 1)
                j = i - 1
                if 0 <= j < PAIRS:
                    if j == 0:
                        pe.wait_ge(wprep, 2 * HALVES)
                    pe.wait_ge(hT_ok, j + 1)
                    if j >= 1:
                        pe.wait_ge(sr99_ok, j)
                    for e in range(2):
                        for h in range(HALVES):
                            ins = pe.matmul(dB[0][:, 4 * e:4 * e + 4], hT[:, j % 2, h, e * P:(e + 1) * P],
                                            w4[:, h, :], start=(h == 0), stop=(h == HALVES - 1))
                    ins.then_inc(proj, 1)
                j = i - 2
                if 0 <= j < PAIRS:
                    pe.wait_ge(diag_ok, j + 1)
                    if j >= 1:
                        pe.wait_ge(sl_ok, j)
                    pe.matmul(dB[1][:, 0:2 * P], ones[:], diag[:].rearrange("p e n -> p (e n)"), start=True,
                              stop=True).then_inc(wide, 1)
                j = i - 2
                if 0 <= j < PAIRS:
                    for n, (u0, u1) in enumerate(TURNS):
                        if j == u0:
                            pe.wait_ge(tr_part if u1 < PAIRS else tr_done, n + 1 if u1 < PAIRS else 1)
                    pe.wait_ge(h1_ok[0], j + 1)
                    pe.wait_ge(h2_ok, j + 1)
                    for v in range(2):
                        for h in range(HALVES):
                            ins = adj_turned(j, v, h)
                            if j == PAIRS - 1 and v == 1:
                                ins.then_inc(a_done, 1)
                j = i - 5
                if 0 <= j < PAIRS:
                    unit(0, j)

            def adj_part(m, h, u0=0, u1=PAIRS):
                if h == 0:
                    pe.wait_ge(tr_done, m + 1)
                if u0 == 0:
                    pe.wait_ge(ta2_ok, 2 * m + (h - 1))
                for u in range(u0, u1):
                    for v in range(2):
                        ins = adj_turned(u, v, h)
                if u1 == PAIRS:
                    ins.then_inc(a_done, 1)

            def dense_b(m, first=False):
                pe.wait_ge(ta2_ok, 2 * m + 2)
                if not first:
                    pe.wait_ge(ub_ok, 2 * m)
                for e in range(2):
                    rows = slice(e * P, (e + 1) * P)
                    ins = dense(dB[e][:, 0:HW], lambda h: Ta[:, 0, h, rows], lambda h: Ta[:, 1, h, rows], w16[1])
                ins.then_inc(db_ok, 1)

            def turn_e(q, first=False):
                pe.wait_ge(ae_ok, 2 * q + 2)
                if not first:
                    pe.wait_ge(te2_ok, q)
                transposes(tp, AE).then_inc(tp_w, 1)

            def dense_a(q, first=False):
                pe.wait_ge(te2_ok, q + 1)
                if not first:
                    pe.wait_ge(wm_ok, 2 * q)
                for e in range(2):
                    ins = dense(dA[:, e * D:(e + 1) * D], lambda h: Te[:, 0, e, h], lambda h: Te[:, 1, e, h], w16[0])
                ins.then_inc(da_ok, 1)

            def layer0(m, q, first=False):
                adj_part(m, 0)
                adj_part(m, 1, 0, 7)
                turn_e(q, first)
                adj_part(m, 1, 7)
                if not first:
                    dense_a(q)
                for u in range(PAIRS):
                    unit(m, u)
                    if u == 0 and first:
                        dense_a(q, True)
                    if u == 9:
                        dense_b(m)

            pe.wait_ge(w16b, 3)
            pe.wait_ge(sr99_ok, PAIRS)
            pe.wait_ge(sl_ok, PAIRS)
            dense_b(0, True)
            layer0(1, 0, True)
            with pe.Fori(1, PAIRS - 1) as q:
                layer0(q + 1, q)

            def units(g, u0, u1):
                pe.wait_ge(h2_ok, PAIRS + u1)
                pe.wait_ge(h1_ok[1], u1)
                for u in range(u0, u1):
                    for v in range(2):
                        for e in range(2):
                            ins = adj_tile(u, v, e)
                if u1 == AGROUPS[g][1]:
                    ins.then_inc(grp_done[g], 1)

            def group(m, g):
                pe.wait_ge(adj_ld[g], 16 * m + 16)
                units(g, *AGROUPS[g])

            def turn_p(q):
                pe.wait_ge(pool_ok, 2 * q + 2)
                transposes(tp, AE).then_inc(l1t_w, 1)

            def dense_p(q):
                pe.wait_ge(l1t_2, q + 1)
                for e in range(2):
                    ins = dense(dA[:, e * D:(e + 1) * D], lambda h: Te[:, 0, e, h], lambda h: Te[:, 1, e, h], w16[2])
                ins.then_inc(l1d_ok, 1)

            pe.wait_ge(ta2_ok, TILES)
            pe.wait_ge(adj_ld[0], 16)
            units(0, 0, 2)
            turn_e(PAIRS - 1)
            units(0, 2, 4)
            dense_a(PAIRS - 1)
            group(0, 1)
            pe.wait_ge(adj_ld[2], 16)
            units(2, 8, PAIRS - 1)
            units(2, PAIRS - 1, PAIRS)
            def layer1(q, first=False):
                pe.wait_ge(pt_c, 2 * q + 2)
                group(q + 1, 0)
                turn_p(q)
                group(q + 1, 1)
                group(q + 1, 2)
                if not first:
                    pe.wait_ge(o_ok, q)
                dense_p(q)

            layer1(0, True)
            with pe.Fori(1, PAIRS - 2) as q:
                layer1(q)

            def tile_units(e, u0, u1):
                for u in range(u0, u1):
                    for v in range(2):
                        ins = adj_tile(u, v, e)
                if u1 == PAIRS:
                    ins.then_inc(half_done, 1)

            def turn_tile(e):
                pe.wait_ge(pool_ok, 2 * last + (e + 1))
                for h in range(HALVES):
                    ins = pe.transpose(dB[e][:, h * P:(h + 1) * P], AE[:, e, h * P:(h + 1) * P], ident[:])
                ins.then_inc(end_t, 1)

            def dense_tile(e):
                pe.wait_ge(end_2, e + 1)
                dense(accE[e][:, 0:D], lambda h: Ta[:, 0, e, h * P:(h + 1) * P],
                      lambda h: Ta[:, 1, e, h * P:(h + 1) * P], w16[2]).then_inc(end_d, 1)

            last = PAIRS - 1
            pe.wait_ge(pt_c, 2 * last)
            for g, (u0, u1) in enumerate(AGROUPS):
                pe.wait_ge(adj_ld[g], 16 * PAIRS)
                tile_units(0, u0, u1)
                if g == 0:
                    turn_p(last - 1)
            pe.wait_ge(o_ok, last - 1)
            dense_p(last - 1)
            tile_units(1, 0, 7)
            turn_tile(0)
            tile_units(1, 7, 10)
            dense_tile(0)
            tile_units(1, 10, PAIRS)
            turn_tile(1)
            dense_tile(1)

        @block.vector
        def _(dve):
            dve.memset(stage[96:P, :, :, QN - 1:QN], 0.0).then_inc(pads, 1)
            dve.memset(xs[96:P, TILES - 1, :], 0.0).then_inc(pads, 1)
            dve.memset(bias4[:, :, 0:1], 0.0)
            dve.memset(bias4[:, :, 3:4], 0.0).then_inc(bias_pad, 1)

            def pair_stats(i, slot, par, l, src):
                if l:
                    dve.wait_ge(nmr_ok[0], len(BATCHES))
                    dve.wait_ge(x1_ok, i + 1)
                for e in range(2):
                    ins = dve.bn_stats(bst[:, par, e], src[:, e])
                ins.then_inc(bnr[l], 1)
                if l:
                    dve.wait_ge(nmr_ok[0], len(BATCHES))
                dve.wait_ge(bnr[l], i + 1)
                for e in range(2):
                    ins = dve.bn_aggr(mv[:, slot, e], bst[:, par, e])
                ins.then_inc(stats[l], 1)

            def minus_mean(a, b, l, count):
                dve.wait_ge(rstd_ok[l], count)
                dve.scalar_tensor_tensor(out=nmr[:, a:b], in0=mv[:, a:b, :, 0], scalar=-1.0, in1=rstd[:, a:b],
                                         op0=ALU.mult, op1=ALU.mult).then_inc(nmr_ok[l], 1)

            def batch_nmr(n):
                minus_mean(*BATCHES[n], 0, n + 1)

            def pair_nmr(q):
                minus_mean(0, 1, 1, q + 1)

            def second_part(i, par, l, first, dst):
                dve.wait_ge(h1_ok[l], i + 1)
                dve.tensor_tensor(dst, hf[:, par], first, ALU.subtract).then_inc(h2_ok, 1)

            def turn_adj(u0=0, u1=PAIRS, part=None):
                for e in range(2):
                    src = stage[:, e].bitcast(U32).rearrange("p b (u r) -> p b u r", r=QUAD)[:, :, u0:u1]
                    dst = adjT[:, u0:u1, e].rearrange("p u (b c) v -> p b u (c v)", b=4).bitcast(U32)
                    ins = dve.transpose(dst, src)
                if u1 == PAIRS:
                    ins.then_inc(tr_done, 1)
                elif part is not None:
                    ins.then_inc(part, 1)

            def weights():
                dve.wait_ge(w_in, 16 * N_WDMA)
                for h in range(HALVES):
                    for k, dst in enumerate((w4[:, h, 3:4], w4[:, h, 0:1])):
                        dve.tensor_tensor_reduce(out=prod[:, 2 * h + k], in0=wsa[:, h, :], in1=arep[:, k * D:(k + 1) * D],
                                                 scale=1.0, scalar=0.0, op0=ALU.mult, op1=ALU.add,
                                                 accum_out=dst).then_inc(wprep, 1)

            def mask(m, u):
                dve.wait_ge(exp_ok, m * PAIRS + (u + 1))
                for v in range(2):
                    t = 2 * u + v
                    rows = adjT[:, u, :, :, v].rearrange("p e i -> p (e i)")
                    ins = dve.scalar_tensor_tensor(out=Z[:, u, v], in0=rows, scalar=vr[:, t:t + 1], in1=Z[:, u, v],
                                                   op0=ALU.mult, op1=ALU.mult)
                ins.then_inc(mask_ok, 1)

            def split(m, u):
                dve.wait_ge(mask_ok, m * PAIRS + (u + 1))
                hi = Z[:, u].bitcast(BF16).rearrange("p v (i w) -> p v i w", w=2)[:, :, :, 1]
                dve.tensor_tensor(E2[:, u], Z[:, u], hi, ALU.subtract).then_inc(e2_ok, 1)

            def first_stats(i):
                g = [g for g, (a, b) in enumerate(GROUPS) if a <= i < b][0]
                dve.wait_ge(x_in[g], 16 * (4 if g < len(GROUPS) - 1 else 6))
                if i >= 2:
                    dve.wait_ge(stats[0], i - 1)
                pair_stats(i, i, i % 2, 0, xs[:, 2 * i:2 * i + 2])

            def largest_weights():
                dve.wait_ge(w2_in, 16 * N_W2DMA)
                for k, w in enumerate((wsa, wg, w1)):
                    dve.tensor_reduce(out=wabs[:, k:k + 1], in_=w[:].rearrange("p h n -> p (h n)"),
                                      axis=mybir.AxisListType.X, op=ALU.max,
                                      apply_absolute_value=True).then_inc(wabs_ok, 1)
                dve.wait_ge(wabs_ok, 3)
                for k in range(3):
                    ins = dve.tensor_scalar(wdiag[:, k], ident[:], wabs[:, k:k + 1], None, ALU.mult)
                ins.then_inc(wdiag_ok, 1)

            def weight_scales():
                dve.wait_ge(wspread, 1)
                dve.tensor_reduce(out=wmax0[:], in_=accE[0][:, 0:3 * P].rearrange("p (k n) -> p k n", k=3),
                                  axis=mybir.AxisListType.X, op=ALU.max).then_inc(wmax_c, 1)
                dve.wait_ge(wmax_c, 1)
                dve.tensor_scalar(wmax[:], wmax0[:], 1e-30, None, ALU.max).then_inc(wmax_c, 1)
                dve.wait_ge(wmax_c, 2)
                dve.reciprocal(winv[:], wmax[:]).then_inc(winv_ok, 1)

            def second_weights(k):
                dve.wait_ge(w16a, k + 1)
                dve.wait_ge(winv_ok, 1)
                dve.scalar_tensor_tensor(out=w16[k][:, 1], in0=(wsa, wg, w1)[k][:], scalar=winv[:, k:k + 1],
                                         in1=w16[k][:, 0], op0=ALU.mult, op1=ALU.subtract).then_inc(w16b, 1)

            first_stats(0)
            first_stats(1)
            batch_nmr(0)
            batch_nmr(1)
            weights()
            for i in range(PAIRS + 4):
                if i in (1, 3, 6):
                    batch_nmr({1: 2, 3: 3, 6: 4}[i])
                for j in (2 * i + 2, 2 * i + 3):
                    if j < PAIRS:
                        first_stats(j)
                j = i - 2
                if 0 <= j < PAIRS:
                    dve.wait_ge(proj, j + 1)
                    if j == 0:
                        dve.wait_ge(bias_pad, 1)
                        dve.wait_ge(bias_in, 64)
                    taken = dB[0][:, 0:8].rearrange("p (e k) -> p e k", k=4)
                    dve.tensor_tensor(srw[:, 2 * j:2 * j + 2, :], taken, bias4[:], ALU.add).then_inc(srw_ok, 1)
                    dve.tensor_scalar(sr99[:, 2 * j:2 * j + 2], taken[:, :, 0], 1.0 - SLOPE, None,
                                      ALU.mult).then_inc(sr99_ok, 1)
                    dve.wait_ge(srw_ok, j + 1)
                    if j >= 1:
                        dve.wait_ge(wide, j)
                    for e in range(2):
                        ins = dve.tensor_scalar(diag[:, e], ident[:], srw[:, 2 * j + e, 3:4], None, ALU.mult)
                    ins.then_inc(diag_ok, 1)
                j = i - 1
                if 0 <= j < PAIRS:
                    second_part(j, j % 2, 0, h1[0][:, 2 * j:2 * j + 2, 0:D], h2[0][:, 2 * j:2 * j + 2])
                if 1 <= i < 1 + len(TURNS):
                    if i == 1:
                        dve.wait_ge(adj_in, 16 * 4)
                    turn_adj(*TURNS[i - 1], tr_part)
                if i == 3:
                    largest_weights()
                if i == 4:
                    weight_scales()
                if 7 <= i < 10:
                    second_weights(i - 7)
                j = i - 4
                if 0 <= j < PAIRS:
                    dve.wait_ge(vr_ok, j + 1)
                    if j == 0:
                        dve.wait_ge(tr_done, 1)
                    mask(0, j)
                    split(0, j)
                    if j == 5:
                        dve.wait_ge(adj_in, 16 * 8)
                        dve.wait_ge(stored, 16)
                    if j >= 5:
                        u0, u1 = {5: (0, 2), 6: (2, 4), 7: (4, 6)}.get(j, (j - 2, j - 1))
                        dve.wait_ge(unit_done, u1)
                        turn_adj(u0, u1)
            def second_sums(m, h):
                dve.wait_ge(th_ok, 2 * m + (h + 1))
                dve.tensor_tensor(Ta[:, 1, h], accA[h][:, 0:2 * P], Ta[:, 0, h], ALU.subtract).then_inc(ta2_ok, 1)

            def second_turned(count, done, ok):
                dve.wait_ge(done, count)
                dve.tensor_tensor(Te[:, 1].rearrange("p e h i -> p (e h i)"), tp[:],
                                  Te[:, 0].rearrange("p e h i -> p (e h i)"), ALU.subtract).then_inc(ok, 1)

            for h in range(HALVES):
                second_sums(0, h)
            for u in (PAIRS - 2, PAIRS - 1):
                dve.wait_ge(unit_done, u + 1)
                turn_adj(u, u + 1)

            def row_sums(q):
                dve.wait_ge(unit_done, q * PAIRS + PAIRS)
                for e in range(2):
                    ins = dve.scalar_tensor_tensor(out=ssum[:, e:e + 1], in0=el[:, bass.ds(2 * q + e, 1)],
                                                   scalar=SUM_EPS, in1=accE[e][:, ones_col:ones_col + 1],
                                                   op0=ALU.mult, op1=ALU.add)
                ins.then_inc(rs_c, 1)
                dve.wait_ge(rs_c, q + 1)
                dve.reciprocal(rs[:], ssum[:]).then_inc(rs_ok, 1)

            def gate_args(q):
                dve.wait_ge(db_ok, q + 1)
                for e in range(2):
                    ins = dve.scalar_tensor_tensor(out=zg[:, e:e + 1],
                                                   in0=dB[e][:, D:HW].rearrange("p (a k) -> p a k", a=1),
                                                   scalar=wmax[:, 1:2], in1=srw[:, bass.ds(2 * q + e, 1), 1:3],
                                                   op0=ALU.mult, op1=ALU.add)
                ins.then_inc(zg_ok, 1)

            def gates(q):
                dve.wait_ge(eg_ok, q + 1)
                dve.tensor_scalar(eg1[:], eg[:], 1.0, None, ALU.add).then_inc(gate_c, 1)
                dve.wait_ge(gate_c, q + 1)
                dve.reciprocal(gate[:], eg1[:]).then_inc(gate_ok, 1)
                dve.wait_ge(gate_ok, q + 1)
                dve.tensor_tensor(gscale[:], gate[:], bass.AP(wmax[:].tensor, 0, [[3, P], [0, 2], [1, 2]]),
                                  ALU.mult).then_inc(gscale_ok, 1)

            def mix(q):
                dve.wait_ge(ub_ok, 2 * q + 2)
                dve.wait_ge(w2_in, 16 * N_W2DMA)
                for e in range(2):
                    dve.scalar_tensor_tensor(out=wm[:, e], in0=bgrep[:], scalar=gate[:, e, 1:2], in1=ub[:, e],
                                             op0=ALU.mult, op1=ALU.add).then_inc(wm_c, 1)
                dve.wait_ge(da_ok, q + 1)
                for e in range(2):
                    dve.wait_ge(wm_c, 2 * q + (e + 1))
                    dve.scalar_tensor_tensor(out=wm[:, e], in0=dA[:, e * D:(e + 1) * D],
                                             scalar=gscale[:, e, 0:1], in1=wm[:, e], op0=ALU.mult,
                                             op1=ALU.add).then_inc(wm_ok, 1)

            def residual(q):
                dve.wait_ge(h2_ok, PAIRS + q)
                dve.wait_ge(wx_ok, q + 1)
                dve.tensor_scalar(wm[:], wx[:], 0.5, 0.5, ALU.mult, ALU.add).then_inc(x1_c, 1)
                dve.wait_ge(x1_c, q + 1)
                dve.tensor_tensor(xs[:, bass.ds(2 * q, 2)], xs[:, bass.ds(2 * q, 2)], wm[:],
                                  ALU.add).then_inc(x1_ok, 1)
                pair_stats(q, 0, 0, 1, xs[:, bass.ds(2 * q, 2)])

            def later_second(q):
                second_part(q, 0, 1, h1[1][:, bass.ds(2 * q, 2), 0:D], h2[1][:, bass.ds(2 * q, 2)])

            def next_adj(m, adj_count):
                dve.wait_ge(adj_in, adj_count)
                dve.wait_ge(a_done, 2 * m)
                dve.wait_ge(stored, 16 * m)
                dve.wait_ge(mask_ok, m * PAIRS)
                turn_adj()

            def layer0(m, q, p, adj_count, sums_at=8, turn_at=PAIRS):
                dve.wait_ge(tr_done, m + 1)
                for u in range(PAIRS + 1):
                    if u < PAIRS:
                        mask(m, u)
                    if u >= 1:
                        split(m, u - 1)
                    if p is not None:
                        if u == 1:
                            pair_nmr(p)
                        if u == 9:
                            later_second(p)
                    if u == sums_at:
                        row_sums(q)
                        gate_args(q)
                    if u == sums_at + 2:
                        gates(q)
                    if u == turn_at:
                        second_sums(m, 0)
                        second_turned(q + 1, tp_ev, te2_ok)
                second_sums(m, 1)
                mix(q)
                if adj_count is not None:
                    next_adj(m + 1, adj_count)
                residual(q)

            dve.wait_ge(vr_ok, PAIRS + 1)
            layer0(1, 0, None, 64 * 3, 0, 7)
            with dve.Fori(0, PAIRS - 4) as q:
                layer0(q + 2, q + 1, q, q * 64 + 256)
            last = PAIRS - 1
            layer0(last - 1, last - 2, last - 3, 64 * PAIRS + 128)
            layer0(last, last - 1, last - 2, None)
            pair_nmr(last - 1)
            row_sums(last)
            gate_args(last)
            later_second(last - 1)
            gates(last)
            second_turned(last + 1, tp_ev, te2_ok)
            mix(last)
            residual(last)
            pair_nmr(last)
            dve.wait_ge(hf_ok[1], 2 * PAIRS)
            dve.tensor_copy(h1[1][:, 2 * last:2 * last + 2, 0:D], hf[:, 0]).then_inc(h1_ok[1], 1)
            later_second(last)

            def pooled(m, tiles=(0, 1)):
                if tiles == (0, 1):
                    dve.wait_ge(grp_done[-1], m + 1)
                else:
                    dve.wait_ge(half_done, tiles[0] + 1)
                dve.wait_ge(hp_ok, m + 1)
                for e in tiles:
                    dve.tensor_scalar(degm[:, e:e + 1], accA[e][:, ones_col:ones_col + 1], 1.0, None,
                                      ALU.max).then_inc(deg_c, 1)
                for e in tiles:
                    dve.tensor_tensor(wm[:, e], accA[e][:, 0:D], hp[:, e], ALU.add).then_inc(pt_c, 1)
                for e in tiles:
                    dve.wait_ge(deg_c, 2 * m + (e + 1))
                    dve.reciprocal(drp[:, e:e + 1], degm[:, e:e + 1]).then_inc(drp_ok, 1)
                for e in tiles:
                    dve.wait_ge(drp_ok, 2 * m + (e + 1))
                    dve.wait_ge(pt_c, 2 * m + (e + 1))
                    dve.scalar_tensor_tensor(out=AE[:, e], in0=wm[:, e], scalar=drp[:, e:e + 1], in1=hp[:, e],
                                             op0=ALU.mult, op1=ALU.add).then_inc(pool_ok, 1)

            def output(q, first=False):
                dve.wait_ge(l1d_ok, q + 1)
                dve.scalar_tensor_tensor(out=wx[:], in0=dA[:].rearrange("p (e d) -> p e d", e=2),
                                         scalar=wmax[:, 2:3], in1=bass.AP(b1rep[:].tensor, 0, [[D, P], [0, 2], [1, D]]),
                                         op0=ALU.mult, op1=ALU.add).then_inc(ob_c, 1)
                dve.wait_ge(ob_c, q + 1)
                if not first:
                    dve.wait_ge(o_out, 16 * q)
                dve.scalar_tensor_tensor(out=osb[:], in0=wx[:], scalar=0.0, in1=xs[:, bass.ds(2 * q, 2)],
                                         op0=ALU.max, op1=ALU.add).then_inc(o_ok, 1)

            pooled(0)
            second_turned(1, l1t_ev, l1t_2)
            pooled(1)
            output(0, True)
            with dve.Fori(1, PAIRS - 2) as q:
                second_turned(q + 1, l1t_ev, l1t_2)
                pooled(q + 1)
                output(q)
            last = PAIRS - 1
            def second_tile(e):
                dve.wait_ge(end_ev, e + 1)
                dve.tensor_tensor(Ta[:, 1, e], dB[e][:, 0:2 * P], Ta[:, 0, e], ALU.subtract).then_inc(end_2, 1)

            second_turned(last, l1t_ev, l1t_2)
            pooled(last, (0,))
            output(last - 1)
            second_tile(0)
            pooled(last, (1,))
            second_tile(1)
            for e in range(2):
                dve.wait_ge(end_d, e + 1)
                dve.scalar_tensor_tensor(out=wx[:, e], in0=accE[e][:, 0:D], scalar=wmax[:, 2:3], in1=b1rep[:],
                                         op0=ALU.mult, op1=ALU.add).then_inc(ob_c, 1)
                dve.wait_ge(ob_c, last + (e + 1))
                dve.scalar_tensor_tensor(out=ub[:, e], in0=wx[:, e], scalar=0.0, in1=xs[:, 2 * last + e],
                                         op0=ALU.max, op1=ALU.add).then_inc(end_o, 1)


_INS = ['x', 'adj', 'L0_gnn_W_sa', 'L0_gnn_a_sa', 'L0_gnn_W_gcnb', 'L0_gnn_b_gcnb', 'L0_gnn_Wa', 'L0_gnn_ba',
        'L0_gnn_Wb', 'L0_gnn_bb', 'L1_gnn_W', 'L1_gnn_b']


def kernel(**inputs):
    import numpy as _np
    import concourse.bacc as _bacc
    from concourse import mybir as _mybir
    from concourse.bass_utils import run_bass_kernel_spmd as _run

    nc = _bacc.Bacc("TRN2", target_bir_lowering=False, num_devices=1)
    arrays, args = {}, []
    for name in _INS:
        a = _np.ascontiguousarray(inputs[name])
        arrays[f"in_{name}_dram"] = a
        args.append(nc.dram_tensor(f"in_{name}_dram", a.shape, _mybir.dt.from_np(a.dtype), kind="ExternalInput").ap())
    shape = inputs['x'].shape
    args.append(nc.dram_tensor("out_0_dram", shape, _mybir.dt.float32, kind="ExternalOutput").ap())
    gnn_kernel(nc, *args)
    r = _run(nc, [arrays], core_ids=[0])
    return r.results[0]["out_0_dram"]
```
